# Optimizing a Trainium2 kernel written in Bass

```python
import numpy as np
import jax
import jax.numpy as jnp

def _softmax(x, axis=-1):
    return jax.nn.softmax(x, axis=axis)

def _gelu(x):
    return jax.nn.gelu(x, approximate=True)

def _silu(x):
    return jax.nn.silu(x)

def _sigmoid(x):
    return jax.nn.sigmoid(x)

def _layernorm(x, axis=-1, eps=1e-05):
    m = jnp.mean(x, axis=axis, keepdims=True)
    v = jnp.var(x, axis=axis, keepdims=True)
    return (x - m) / jnp.sqrt(v + eps)

def _scatter_add(tgt, idx, src, axis=0):
    return tgt.at[idx].add(src)

def _segment_sum(src, seg, n):
    return jax.ops.segment_sum(src, seg, n)
kernel_name = 'mk_macaron_d1_jaxref_r8_67ffb7'

def setup_inputs(seed: int=0):
    np.random.seed(seed)
    _w = jnp.asarray

    def _L0_attn_setup():
        import jax, jax.numpy as jnp
        import numpy as np
        D_MODEL, D_STATE, D_INNER, DT_RANK, D_CONV = (128, 16, 256, 64, 4)
        B, L = (2, 256)
        key = jax.random.key(seed)
        ks = jax.random.split(key, 10)
        dt_init_std = DT_RANK ** (-0.5)
        dt = jnp.exp(jax.random.uniform(ks[8], (D_INNER,)) * (np.log(0.1) - np.log(0.001)) + np.log(0.001))
        dt = jnp.clip(dt, 0.0001, None)
        inv_dt = dt + jnp.log(-jnp.expm1(-dt))
        s = 0.02
        return {'x': jax.random.normal(ks[0], (B, L, D_MODEL), dtype=jnp.float32), 'W_in': jax.random.normal(ks[1], (D_MODEL, 2 * D_INNER), dtype=jnp.float32) * s, 'conv_w': jax.random.normal(ks[2], (D_INNER, 1, D_CONV), dtype=jnp.float32) * s, 'conv_b': jnp.zeros((D_INNER,), dtype=jnp.float32), 'A_log': jnp.log(jnp.arange(1, D_STATE + 1, dtype=jnp.float32)), 'D': jnp.ones((D_INNER,), dtype=jnp.float32), 'W_x': jax.random.normal(ks[3], (D_INNER, DT_RANK + 2 * D_STATE), dtype=jnp.float32) * s, 'W_dt': jax.random.uniform(ks[4], (DT_RANK, D_INNER), minval=-dt_init_std, maxval=dt_init_std, dtype=jnp.float32), 'b_dt': inv_dt.astype(jnp.float32), 'W_out': jax.random.normal(ks[5], (D_INNER, D_MODEL), dtype=jnp.float32) * s}
    _L0_attn_in = _L0_attn_setup()

    def _L0_ffn_setup():
        import jax, jax.numpy as jnp
        import numpy as np
        HIDDEN = 128
        INTER = 512
        NUM_EXPERTS = 8
        TOP_K = 2
        EPS = 1e-05

        def _layer_norm(x, g, b):
            m = jnp.mean(x, axis=-1, keepdims=True)
            v = jnp.mean(jnp.square(x - m), axis=-1, keepdims=True)
            return (x - m) * jax.lax.rsqrt(v + EPS) * g + b
        key = jax.random.key(seed)
        ks = jax.random.split(key, 8)
        s = 0.02
        return {'x': jax.random.normal(ks[0], (4, 256, HIDDEN), dtype=jnp.float32), 'ln1_g': jnp.ones((HIDDEN,), jnp.float32), 'ln1_b': jnp.zeros((HIDDEN,), jnp.float32), 'attn_w': jax.random.normal(ks[1], (HIDDEN, HIDDEN), jnp.float32) * s, 'ln2_g': jnp.ones((HIDDEN,), jnp.float32), 'ln2_b': jnp.zeros((HIDDEN,), jnp.float32), 'gate_w': jax.random.normal(ks[2], (NUM_EXPERTS, HIDDEN), jnp.float32) * s, 'gate_proj': jax.random.normal(ks[3], (NUM_EXPERTS, INTER, HIDDEN), jnp.float32) * s, 'up_proj': jax.random.normal(ks[4], (NUM_EXPERTS, INTER, HIDDEN), jnp.float32) * s, 'down_proj': jax.random.normal(ks[5], (NUM_EXPERTS, HIDDEN, INTER), jnp.float32) * s}
    _L0_ffn_in = _L0_ffn_setup()
    _d = {'L0_attn_x': _L0_attn_in['x'], 'L0_attn_W_in': _L0_attn_in['W_in'], 'L0_attn_conv_w': _L0_attn_in['conv_w'], 'L0_attn_conv_b': _L0_attn_in['conv_b'], 'L0_attn_A_log': _L0_attn_in['A_log'], 'L0_attn_D': _L0_attn_in['D'], 'L0_attn_W_x': _L0_attn_in['W_x'], 'L0_attn_W_dt': _L0_attn_in['W_dt'], 'L0_attn_b_dt': _L0_attn_in['b_dt'], 'L0_attn_W_out': _L0_attn_in['W_out'], 'L0_ffn_ln1_g': _L0_ffn_in['ln1_g'], 'L0_ffn_ln1_b': _L0_ffn_in['ln1_b'], 'L0_ffn_attn_w': _L0_ffn_in['attn_w'], 'L0_ffn_ln2_g': _L0_ffn_in['ln2_g'], 'L0_ffn_ln2_b': _L0_ffn_in['ln2_b'], 'L0_ffn_gate_w': _L0_ffn_in['gate_w'], 'L0_ffn_gate_proj': _L0_ffn_in['gate_proj'], 'L0_ffn_up_proj': _L0_ffn_in['up_proj'], 'L0_ffn_down_proj': _L0_ffn_in['down_proj']}
    _x0 = _d['L0_attn_x']
    _d['L0_attn_x'] = jax.random.normal(jax.random.fold_in(jax.random.key(seed), 1), (8, 256, 128), dtype=_x0.dtype)
    del _x0
    return _d

def reference(L0_attn_x, L0_attn_W_in, L0_attn_conv_w, L0_attn_conv_b, L0_attn_A_log, L0_attn_D, L0_attn_W_x, L0_attn_W_dt, L0_attn_b_dt, L0_attn_W_out, L0_ffn_ln1_g, L0_ffn_ln1_b, L0_ffn_attn_w, L0_ffn_ln2_g, L0_ffn_ln2_b, L0_ffn_gate_w, L0_ffn_gate_proj, L0_ffn_up_proj, L0_ffn_down_proj):

    def _L0_attn_ref(x, W_in, conv_w, conv_b, A_log, D, W_x, W_dt, b_dt, W_out):
        import jax, jax.numpy as jnp
        import numpy as np
        D_MODEL, D_STATE, D_INNER, DT_RANK, D_CONV = (128, 16, 256, 64, 4)
        B, L = (2, 256)
        length = x.shape[1]
        xz = jnp.einsum('bld,de->ble', x, W_in)
        u, z = jnp.split(xz, 2, axis=-1)
        u_c = u.transpose(0, 2, 1)
        u_c = jax.lax.conv_general_dilated(u_c, conv_w, window_strides=(1,), padding=[(D_CONV - 1, 0)], dimension_numbers=('NCH', 'OIH', 'NCH'), feature_group_count=D_INNER)
        u_c = u_c + conv_b[None, :, None]
        u = jax.nn.silu(u_c.transpose(0, 2, 1))
        x_dbl = jnp.einsum('bld,de->ble', u, W_x)
        dt_lr, b_sel, c_sel = jnp.split(x_dbl, [DT_RANK, DT_RANK + D_STATE], axis=-1)
        dt = jax.nn.softplus(jnp.einsum('blr,rd->bld', dt_lr, W_dt) + b_dt)
        a_diag = -jnp.exp(A_log)

        def step(h, inp):
            dt_t, b_t, c_t, u_t = inp
            a_bar = jnp.exp(dt_t[:, :, None] * a_diag)
            h = a_bar * h + (dt_t * u_t)[:, :, None] * b_t[:, None, :]
            y = jnp.einsum('bdn,bn->bd', h, c_t) + D * u_t
            return (h, y)
        h0 = jnp.zeros((x.shape[0], D_INNER, D_STATE), dtype=x.dtype)
        xs = (dt.transpose(1, 0, 2), b_sel.transpose(1, 0, 2), c_sel.transpose(1, 0, 2), u.transpose(1, 0, 2))
        _, ys = jax.lax.scan(step, h0, xs)
        y = ys.transpose(1, 0, 2)
        return jnp.einsum('bld,de->ble', y * jax.nn.silu(z), W_out)

    def _L0_ffn_ref(x, ln1_g, ln1_b, attn_w, ln2_g, ln2_b, gate_w, gate_proj, up_proj, down_proj):
        import jax, jax.numpy as jnp
        import numpy as np
        HIDDEN = 128
        INTER = 512
        NUM_EXPERTS = 8
        TOP_K = 2
        EPS = 1e-05

        def _layer_norm(x, g, b):
            m = jnp.mean(x, axis=-1, keepdims=True)
            v = jnp.mean(jnp.square(x - m), axis=-1, keepdims=True)
            return (x - m) * jax.lax.rsqrt(v + EPS) * g + b
        B, S, H = x.shape
        h = x + jnp.einsum('bsh,oh->bso', _layer_norm(x, ln1_g, ln1_b), attn_w)
        t = _layer_norm(h, ln2_g, ln2_b).reshape(-1, H)
        T = t.shape[0]
        logits = jnp.einsum('th,eh->te', t, gate_w)
        top_vals, top_idx = jax.lax.top_k(logits, TOP_K)
        rw = jax.nn.softmax(top_vals, axis=-1)
        comb = jnp.zeros((T, NUM_EXPERTS), dtype=t.dtype)
        comb = comb.at[jnp.arange(T)[:, None], top_idx].add(rw)
        out = jnp.zeros_like(t)
        for e in range(NUM_EXPERTS):
            g = jnp.einsum('th,ih->ti', t, gate_proj[e])
            u = jnp.einsum('th,ih->ti', t, up_proj[e])
            oe = jnp.einsum('ti,hi->th', jax.nn.silu(g) * u, down_proj[e])
            out = out + comb[:, e:e + 1] * oe
        return h + out.reshape(B, S, H)
    x = L0_attn_x
    x = x + 0.5 * _L0_ffn_ref(_layernorm(x, axis=-1), L0_ffn_ln1_g, L0_ffn_ln1_b, L0_ffn_attn_w, L0_ffn_ln2_g, L0_ffn_ln2_b, L0_ffn_gate_w, L0_ffn_gate_proj, L0_ffn_up_proj, L0_ffn_down_proj)
    x = x + _L0_attn_ref(_layernorm(x, axis=-1), L0_attn_W_in, L0_attn_conv_w, L0_attn_conv_b, L0_attn_A_log, L0_attn_D, L0_attn_W_x, L0_attn_W_dt, L0_attn_b_dt, L0_attn_W_out)
    x = x + 0.5 * _L0_ffn_ref(_layernorm(x, axis=-1), L0_ffn_ln1_g, L0_ffn_ln1_b, L0_ffn_attn_w, L0_ffn_ln2_g, L0_ffn_ln2_b, L0_ffn_gate_w, L0_ffn_gate_proj, L0_ffn_up_proj, L0_ffn_down_proj)
    return x

_drawn_inputs = setup_inputs


def setup_inputs(seed=0):
    import zlib

    import numpy as np

    out = dict(_drawn_inputs(seed))
    spreads = {'L0_attn_conv_b': (0.0, 0.8),
     'L0_attn_D': (1.0, 0.6),
     'L0_ffn_ln1_g': (1.0, 0.577),
     'L0_ffn_ln1_b': (0.0, 0.581),
     'L0_ffn_ln2_g': (1.0, 0.6),
     'L0_ffn_ln2_b': (0.0, 0.8)}
    factors = {'L0_attn_W_in': 8.0,
     'L0_attn_conv_w': 8.0,
     'L0_attn_A_log': 8.0,
     'L0_attn_W_x': 8.0,
     'L0_attn_W_dt': 8.0,
     'L0_attn_b_dt': 8.0,
     'L0_attn_W_out': 8.0,
     'L0_ffn_gate_w': 8.0,
     'L0_ffn_gate_proj': 8.0,
     'L0_ffn_up_proj': 8.0,
     'L0_ffn_down_proj': 8.0}
    for name, (base, spread) in spreads.items():
        noise = np.random.default_rng([zlib.crc32(name.encode()), seed]).standard_normal(out[name].shape)
        drawn = base * np.exp(spread * noise) if base else spread * noise
        out[name] = jnp.asarray(drawn.astype(out[name].dtype))
    for name, factor in factors.items():
        out[name] = (out[name] * factor).astype(out[name].dtype)
    return out
```

```python
from contextlib import ExitStack

import concourse.bass as bass
from concourse import mybir

ALU = mybir.AluOpType
ACT = mybir.ActivationFunctionType
F32 = mybir.dt.float32
BF16 = mybir.dt.bfloat16
U32 = mybir.dt.uint32

P = 128
D = 128
NT = 16
GT = 4
NG = NT // GT
GW = GT * P
NE = 8
FI = 512
NI = FI // P
DI = 256
NH = DI // P
NB = 8
L = 256
GB = GW // L
NS = 16
DR = 64
KC = 4
EPS = 1e-5
STEPS = NT * NE
AHEAD = 2


def macaron(nc, a, out):
    ctx = ExitStack()
    with ctx:
        def sb(name, shape, dt=F32):
            return ctx.enter_context(nc.sbuf_tensor(name, shape, dt))

        def sem(name):
            return ctx.enter_context(nc.semaphore(name))

        bank = ctx.enter_context(nc.psum_tensor("bank", [P, 8, 512], F32))
        x = sb("x", [P, NT, D])
        normed = sb("normed", [P, NT, D])
        x0 = sb("x0", [P, NT, D])
        hid = sb("hid", [P, NT, D])
        aT = sb("aT", [P, NT * P])
        tT = sb("tT", [P, NT * P])
        gate_w = sb("gate_w", [P, NE, FI])
        up_w = sb("up_w", [P, NE, FI])
        down_w = sb("down_w", [P, NE, NI, D])
        attn_w = sb("attn_w", [P, D])
        router_w = sb("router_w", [P, NE])
        ln_cols = sb("ln_cols", [P, 4])
        ident = sb("ident", [P, P])
        iota8 = sb("iota8", [P, NE])
        eps = sb("eps", [P, 1])
        stats = sb("stats", [P, NT, 6])
        mv = sb("mv", [P, NT, 2])
        std = sb("std", [P, NT])
        rstd = sb("rstd", [P, NT])
        logits = sb("logits", [P, NT, NE])
        top = sb("top", [P, NT, 8])
        topi = sb("topi", [P, NT, 8], U32)
        topf = sb("topf", [P, NT, 2])
        gap = sb("gap", [P, NT])
        ew = sb("ew", [P, NT])
        w = sb("w", [P, 2, NT])
        pick = sb("pick", [P, NT, NE])
        comb = sb("comb", [P, NT, NE])
        tile = sb("tile", [P, 2, P])
        sg = sb("sg", [P, 2, FI])
        act = sb("act", [P, 2, FI])
        actT = sb("actT", [P, 2, FI])
        w_in = sb("w_in", [P, 2 * DI])
        conv_w = sb("conv_w", [P, NH, KC])
        cols = sb("cols", [P, 3, NH])
        w_dtlr = sb("w_dtlr", [P, NH, DR])
        w_bc = sb("w_bc", [P, NH, 3 * 2 * NS])
        w_dt = sb("w_dt", [DR, DI])
        w_out = sb("w_out", [P, NH, D])
        a_col = sb("a_col", [P, NS])
        u_raw = sb("u_raw", [P, NH, NB, L + KC - 1])
        dt = u_raw[:].rearrange("p h b l -> p (h b l)")[:, 0:NH * NB * L].rearrange("p (h b l) -> p h b l", h=NH, b=NB)
        u = sb("u", [P, NH, NB, L])
        zs = sb("zs", [P, NH, NT * P])
        dtu = sb("dtu", [P, NH, NT * P])
        dtlr = sb("dtlr", [DR, NT * P])
        bc_hi = sb("bc_hi", [96, NT * P], BF16)
        bc_mid = sb("bc_mid", [96, GW], BF16)
        bc_r1, bc_r2 = actT[0:96, 0, :], actT[0:96, 1, :]
        sel = sb("sel", [96, 2 * NS, P], BF16)
        sp_relu, sp_tmp = sg, act
        sp_exp = aT[:, 0:2 * GW].rearrange("p (s n) -> p s n", s=2)
        sp_ln = aT[:, 2 * GW:4 * GW].rearrange("p (s n) -> p s n", s=2)
        yg = aT[:, 0:NH * GW].rearrange("p (s n) -> p s n", s=NH)

        def scan_buffer(t):
            return t[:].rearrange("p a b -> p (a b)").rearrange("p (s n) -> p s n", s=2)
        decay = scan_buffer(normed)
        drive = scan_buffer(x0)
        state = scan_buffer(hid)
        read = tT[:].rearrange("p (s n) -> p s n", s=2)

        x_in = sem("x_in"); small_in = sem("small_in"); big_in = sem("big_in"); mamba_in = sem("mamba_in")
        out_sent = sem("out_sent")
        consts = sem("consts"); pool_step = sem("pool_step")
        dve_step = sem("dve_step"); act_step = sem("act_step")
        var_ready = sem("var_ready"); std_ready = sem("std_ready"); normed_ready = sem("normed_ready")
        turned = sem("turned"); turned_used = sem("turned_used")
        attn_ready = sem("attn_ready"); attn_used = sem("attn_used")
        logits_ready = sem("logits_ready"); gap_ready = sem("gap_ready"); ew_ready = sem("ew_ready")
        tile_ready = sem("tile_ready"); gu_ready = sem("gu_ready"); silu_done = sem("silu_done")
        mul_done = sem("mul_done"); turn_done = sem("turn_done"); evac_done = sem("evac_done")
        down_done = sem("down_done"); acc_done = sem("acc_done")
        x_ready = sem("x_ready")
        uz_ready = sem("uz_ready"); uz_used = sem("uz_used")
        conv_done = sem("conv_done"); u_ready = sem("u_ready")
        bcx_ready = sem("bcx_ready"); bc_split = sem("bc_split"); dtlr_ready = sem("dtlr_ready")
        dtx_ready = sem("dtx_ready"); dtx_used = sem("dtx_used"); sp_ready = sem("sp_ready"); x_added = sem("x_added")
        dt_ready = sem("dt_ready"); zero_ready = sem("zero_ready"); decay_begun = sem("decay_begun")
        bc_ready = sem("bc_ready"); decay_ready = sem("decay_ready"); drive_done = sem("drive_done")
        scan_done = sem("scan_done"); read_done = sem("read_done"); y_added = sem("y_added")
        yg_ready = sem("yg_ready"); y_used = sem("y_used"); proj_ready = sem("proj_ready")

        block = ctx.enter_context(nc.Block())

        LN_RUNS = 2 + 2 + 1 + 2
        FFN_LN = [[0, 1, 2], [4, 5, 6]]
        MAMBA_LN = 3
        TURN = {1: 0, 2: 1, 3: 2, 5: 3, 6: 4}

        @block.sync
        def _(sp):
            sp.dma_start(x[:], a["x"].rearrange("(t p) d -> p t d", p=P)).then_inc(x_in, 16)
            sp.dma_start(ln_cols[:], a["ln_cols"]).then_inc(small_in, 16)
            sp.dma_start(attn_w[:], a["attn_w"]).then_inc(small_in, 16)
            sp.dma_start(router_w[:], a["router_w"]).then_inc(small_in, 16)
            sp.dma_start(gate_w[:], a["gate_w"]).then_inc(big_in, 16)
            sp.dma_start(up_w[:], a["up_w"]).then_inc(big_in, 16)
            sp.dma_start(down_w[:], a["down_w"]).then_inc(big_in, 16)
            sp.dma_start(w_in[:], a["w_in"]).then_inc(mamba_in, 16)
            sp.dma_start(conv_w[:], a["conv_w"]).then_inc(mamba_in, 16)
            sp.dma_start(cols[:], a["cols"]).then_inc(mamba_in, 16)
            sp.dma_start(w_dtlr[:], a["w_dtlr"]).then_inc(mamba_in, 16)
            sp.dma_start(w_bc[:], a["w_bc"]).then_inc(mamba_in, 16)
            sp.dma_start(w_dt[:], a["w_dt"]).then_inc(mamba_in, 16)
            sp.dma_start(w_out[:], a["w_out"]).then_inc(mamba_in, 16)
            sp.dma_start(a_col[:], a["A_log"].partition_broadcast(P)).then_inc(mamba_in, 16)
            sp.wait_ge(x_ready, 3)
            sp.dma_start(out.rearrange("(t p) d -> p t d", p=P), x[:]).then_inc(out_sent, 16)
            sp.wait_ge(out_sent, 16)
        MAMBA_LOADS = 16 * 8

        @block.gpsimd
        def _(pool):
            g = nc.gpsimd
            g.memset(ident[:], 0.0).then_inc(pool_step, 1)
            g.memset(sel[:], 0.0).then_inc(pool_step, 1)
            g.memset(eps[:], EPS).then_inc(consts, 1)
            g.iota(iota8[:], [[1, NE]], base=0, channel_multiplier=0, allow_small_or_imprecise_dtypes=True).then_inc(consts, 1)
            g.memset(u_raw[:, :, :, 0:KC - 1], 0.0).then_inc(consts, 1)
            pool.wait_ge(pool_step, 2)
            g.affine_select(out=ident[:], in_=ident[:], compare_op=ALU.not_equal, fill=1.0, base=0,
                            pattern=[[-1, P]], channel_multiplier=1).then_inc(consts, 1)
            for part in range(3):
                ins = g.affine_select(out=sel[:], in_=sel[:], compare_op=ALU.not_equal, fill=1.0, base=-32 * part,
                                      pattern=[[-1, 2 * NS], [0, P]], channel_multiplier=1)
                if part < 2:
                    ins.then_inc(pool_step, 1)
                    pool.wait_ge(pool_step, 3 + part)
                else:
                    ins.then_inc(consts, 1)

            def token_tiles(r):
                base = STEPS * r

                def copy(t, parity, free):
                    if free is not None:
                        pool.wait_ge(gu_ready, free)
                    g.tensor_copy(tile[:, parity, :], tT[:, bass.ts(t, P)]).then_inc(tile_ready, 1)
                pool.wait_ge(turned_used, NG * (TURN[FFN_LN[r][2]] + 1))
                for t in range(2):
                    copy(t, t, base - NE * (2 - t) + NE if r else None)
                with pool.Fori(1, NT // 2) as tt:
                    for k in range(2):
                        copy(2 * tt + k, k, (2 * tt + k) * NE + (base - NE))

            token_tiles(0)
            pool.wait_ge(turned, NG * (TURN[MAMBA_LN] + 1))
            g.memset(decay.rearrange("p s (b l) -> p s b l", l=L)[:, :, :, 0:1], 0.0).then_inc(zero_ready, 1)
            steps = 2
            steps = 4
            for q in range(NG * NH):
                gq, h = q // NH, q % NH
                s = q % 2
                e, l, r, t = sp_exp[:, s, :], sp_ln[:, s, :], sp_relu[:, s, :], sp_tmp[:, s, :]
                d = dt[:, h, GB * gq:GB * (gq + 1), :].rearrange("p b l -> p (b l)")
                uq = u[:, h, GB * gq:GB * (gq + 1), :].rearrange("p b l -> p (b l)")
                pool.wait_ge(sp_ready, q + 1)
                for ins in (lambda: g.tensor_scalar(t, e, 1.0, 1.0, ALU.add, ALU.subtract),
                            lambda: g.tensor_tensor(t, e, t, ALU.subtract),
                            lambda: g.tensor_tensor(t, t, l, ALU.add),
                            lambda: g.tensor_tensor(d, t, r, ALU.add)):
                    ins().then_inc(pool_step, 1)
                    steps += 1
                    pool.wait_ge(pool_step, steps)
                g.tensor_tensor(dtu[:, h, bass.ts(gq, GW)], d, uq, ALU.mult).then_inc(dt_ready, 1)
            token_tiles(1)

        @block.scalar
        def _(eng):
            s = nc.scalar

            def std_of(k):
                eng.wait_ge(var_ready, k + 1)
                s.activation(std[:], mv[:, :, 1], ACT.Sqrt, bias=eps[:, 0:1]).then_inc(std_ready, 1)

            def turned_out(k, dst, scale, bias):
                for g in range(NG):
                    n = NG * TURN[k] + g
                    eng.wait_ge(turned, n + 1)
                    s.activation(dst[:, bass.ts(g, GW)], bank[:, n % 2, :], ACT.Identity, bias=bias, scale=scale)\
                        .then_inc(turned_used, 1)

            def ffn(r):
                base = STEPS * r
                std_of(FFN_LN[r][0])
                std_of(FFN_LN[r][1])
                turned_out(FFN_LN[r][1], aT, ln_cols[:, 0:1], ln_cols[:, 1:2])
                std_of(FFN_LN[r][2])
                turned_out(FFN_LN[r][2], tT, ln_cols[:, 2:3], ln_cols[:, 3:4])
                eng.wait_ge(gap_ready, r + 1)
                s.activation(ew[:], gap[:], ACT.Exp).then_inc(ew_ready, 1)

                def silu(n, p):
                    eng.wait_ge(gu_ready, n + 1)
                    eng.wait_ge(mul_done, n + 1)
                    s.activation(sg[:, p, :], bank[:, p, :], ACT.Silu).then_inc(silu_done, 1)

                def evac(n, p):
                    eng.wait_ge(turn_done, n + 1 + AHEAD)
                    eng.wait_ge(down_done, n + 1)
                    s.activation(actT[:, p, :], bank[:, 4 + p, :], ACT.Copy).then_inc(evac_done, 1)

                silu(base, 0)
                with eng.Fori(0, NT - 1) as j:
                    for k in range(NE):
                        silu(j * NE + (base + k + 1), (k + 1) % 2)
                        evac(j * NE + (base + k), k % 2)
                for k in range(NE):
                    n = base + STEPS - NE + k
                    if k < NE - 1:
                        silu(n + 1, (k + 1) % 2)
                    evac(n, k % 2)

            eng.wait_ge(consts, 5)
            eng.wait_ge(small_in, 16 * 3)
            eng.sem_inc(silu_done, AHEAD)
            eng.sem_inc(evac_done, AHEAD)
            ffn(0)

            std_of(MAMBA_LN)
            turned_out(MAMBA_LN, aT, 1.0, 0.0)
            eng.wait_ge(mamba_in, MAMBA_LOADS)
            for g in range(NG):
                eng.wait_ge(uz_ready, g + 1)
                for h in range(NH):
                    s.activation(u_raw[:, h, GB * g:GB * (g + 1), KC - 1:],
                                 bank[:, 4 + h, :].rearrange("p (b l) -> p b l", l=L), ACT.Copy)
                    s.activation(u[:, h, GB * g:GB * (g + 1), :].rearrange("p b l -> p (b l)"), bank[:, 4 + h, :],
                                 ACT.Identity, bias=cols[:, 0, h:h + 1], scale=conv_w[:, h, KC - 1:KC])
                for h in range(NH):
                    ins = s.activation(zs[:, h, bass.ts(g, GW)], bank[:, 6 + h, :], ACT.Silu)
                ins.then_inc(uz_used, 1)
            for h in range(NH):
                eng.wait_ge(conv_done, h + 1)
                uh = u[:, h, :, :].rearrange("p b l -> p (b l)")
                s.activation(uh, uh, ACT.Silu).then_inc(u_ready, 1)
            s.activation(a_col[:], a_col[:], ACT.Exp).then_inc(act_step, 1)
            eng.wait_ge(act_step, 1)
            s.activation(a_col[:], a_col[:], ACT.Copy, scale=-1.0).then_inc(act_step, 1)
            for g in range(NG):
                eng.wait_ge(bcx_ready, g + 1)
                s.activation(dtlr[:, bass.ts(g, GW)], bank[0:DR, g % 2, :], ACT.Copy).then_inc(dtlr_ready, 1)
            for q in range(NG * NH):
                h = q % NH
                p = q % 2
                eng.wait_ge(dtx_ready, q + 1)
                if q >= 2:
                    eng.wait_ge(dt_ready, q - 1)
                x_in_bank = bank[:, 4 + q % 4, :]
                s.activation(sp_exp[:, p, :], x_in_bank, ACT.Abs, bias=cols[:, 2, h:h + 1]).then_inc(act_step, 1)
                s.activation(sp_relu[:, p, :], x_in_bank, ACT.Relu, bias=cols[:, 2, h:h + 1]).then_inc(dtx_used, 1)
                eng.wait_ge(act_step, 2 * q + 3)
                s.activation(sp_exp[:, p, :], sp_exp[:, p, :], ACT.Exp, scale=-1.0).then_inc(act_step, 1)
                eng.wait_ge(act_step, 2 * q + 4)
                s.activation(sp_ln[:, p, :], sp_exp[:, p, :], ACT.Ln, bias=1.0).then_inc(sp_ready, 1)
            eng.wait_ge(zero_ready, 1)
            eng.wait_ge(dt_ready, NG * NH)
            eng.sem_inc(decay_ready, AHEAD)
            decay_v = decay.rearrange("p s (h b l) -> p s h b l", h=NH, b=GB)
            with eng.Fori(0, NG) as c:
                for n in range(NS):
                    m = c * NS + n
                    eng.wait_ge(scan_done, m + 1)
                    eng.sem_inc(decay_begun, 1)
                    for h in range(NH):
                        ins = s.activation(decay_v[:, n % 2, h, :, 1:L], dt[:, h, bass.ts(c, GB), 1:L],
                                           ACT.Exp, scale=a_col[:, n:n + 1])
                    ins.then_inc(decay_ready, 1)
            ffn(1)

        @block.tensor
        def _(pe):
            t = nc.tensor

            def turn_group(k, g):
                n = NG * TURN[k] + g
                pe.wait_ge(normed_ready, n + 1)
                if n >= 2:
                    pe.wait_ge(turned_used, n - 1)
                for i in range(GT):
                    ins = t.transpose(bank[:, n % 2, bass.ts(i, P)], normed[:, GT * g + i, :], ident[:])
                ins.then_inc(turned, 1)

            def ffn(r):
                base = STEPS * r
                k1, k2 = FFN_LN[r][1:]
                for g in range(NG):
                    turn_group(k1, g)
                    n = NG * r + g
                    pe.wait_ge(turned_used, NG * TURN[k1] + g + 1)
                    if n >= 2:
                        pe.wait_ge(attn_used, n - 1)
                    for i in range(GT):
                        ins = t.matmul(bank[:, 2 + g % 2, bass.ts(i, P)], aT[:, bass.ts(GT * g + i, P)], attn_w[:],
                                       start=True, stop=True)
                    ins.then_inc(attn_ready, 1)
                for g in range(NG):
                    turn_group(k2, g)
                    pe.wait_ge(turned_used, NG * TURN[k2] + g + 1)
                    for i in range(GT):
                        j = GT * g + i
                        ins = t.matmul(bank[:, 7, bass.ts(j, NE)], tT[:, bass.ts(j, P)], router_w[:],
                                       start=True, stop=True)
                ins.then_inc(logits_ready, 1)
                pe.wait_ge(gap_ready, r + 1)

                def gate_up(n, p, e, q):
                    if e == 0:
                        pe.wait_ge(tile_ready, q)
                    pe.wait_ge(silu_done, n + 1)
                    pe.wait_ge(mul_done, n + 1)
                    t.matmul(bank[:, p, :], tile[:, q_parity(q), :], gate_w[:, e, :], start=True, stop=True)
                    t.matmul(bank[:, 2 + p, :], tile[:, q_parity(q), :], up_w[:, e, :], start=True, stop=True)\
                        .then_inc(gu_ready, 1)
                parity_of = {}

                def q_parity(q):
                    return parity_of["now"]

                def turn(n, p):
                    pe.wait_ge(mul_done, n + 1 + AHEAD)
                    pe.wait_ge(evac_done, n + 1)
                    for i in range(NI):
                        ins = t.transpose(bank[:, 4 + p, bass.ts(i, P)], act[:, p, bass.ts(i, P)], ident[:])
                    ins.then_inc(turn_done, 1)

                def down(n, p, e):
                    pe.wait_ge(evac_done, n + 1 + AHEAD)
                    pe.wait_ge(acc_done, n + 1)
                    for i in range(NI):
                        ins = t.matmul(bank[:, 6 + p, 0:D], actT[:, p, bass.ts(i, P)], down_w[:, e, i, :],
                                       start=(i == 0), stop=(i == NI - 1))
                    ins.then_inc(down_done, 1)

                def step(n, k, tiles, first=False, last=False):
                    k1 = k + 1
                    if not last:
                        parity_of["now"] = (k1 // NE) % 2
                        gate_up(n + 1, k1 % 2, k1 % NE, tiles(k1 // NE))
                    turn(n, k % 2)
                    if not first:
                        down(n - 1, (k - 1) % 2, (k - 1) % NE)

                pe.wait_ge(big_in, 16 * 3)
                t0 = NT * r
                parity_of["now"] = 0
                gate_up(base, 0, 0, t0 + 1)
                for k in range(NE):
                    step(base + k, k, lambda d: t0 + d + 1, first=(k == 0))
                with pe.Fori(0, NT // 2 - 1) as jj:
                    for k in range(NE, 3 * NE):
                        step(jj * (2 * NE) + (base + k), k, lambda d: jj * 2 + (t0 + d + 1))
                for k in range(NE):
                    kk = STEPS - NE + k
                    step(base + kk, kk, lambda d: t0 + d + 1, last=(k == NE - 1))
                down(base + STEPS - 1, (STEPS - 1) % 2, NE - 1)

            pe.wait_ge(consts, 5)
            pe.wait_ge(small_in, 16 * 3)
            pe.sem_inc(turn_done, AHEAD)
            pe.sem_inc(down_done, AHEAD)
            ffn(0)

            for g in range(NG):
                turn_group(MAMBA_LN, g)
            pe.wait_ge(mamba_in, MAMBA_LOADS)
            for g in range(NG):
                pe.wait_ge(turned_used, NG * TURN[MAMBA_LN] + g + 1)
                if g == 0:
                    pe.wait_ge(x_ready, 1)
                else:
                    pe.wait_ge(uz_used, g)
                for q in range(2 * NH):
                    ins = t.matmul(bank[:, 4 + q, :], w_in[:, bass.ts(q, P)], aT[:, bass.ts(g, GW)], start=True, stop=True)
                ins.then_inc(uz_ready, 1)
            pe.wait_ge(u_ready, NH)
            for g in range(NG):
                if g >= 2:
                    pe.wait_ge(dtlr_ready, g - 1)
                    pe.wait_ge(bc_split, g - 1)
                for h in range(NH):
                    t.matmul(bank[0:DR, g % 2, :], w_dtlr[:, h, :], u[:, h, GB * g:GB * (g + 1), :].rearrange("p b l -> p (b l)"),
                             start=(h == 0), stop=(h == NH - 1))
                for h in range(NH):
                    ins = t.matmul(bank[0:96, 2 + g % 2, :], w_bc[:, h, :], u[:, h, GB * g:GB * (g + 1), :].rearrange("p b l -> p (b l)"),
                                   start=(h == 0), stop=(h == NH - 1))
                ins.then_inc(bcx_ready, 1)
            pe.wait_ge(uz_used, NG)
            for q in range(NG * NH):
                pe.wait_ge(dtlr_ready, q // NH + 1)
                if q >= 4:
                    pe.wait_ge(dtx_used, q - 3)
                t.matmul(bank[:, 4 + q % 4, :], w_dt[:, bass.ts(q % NH, P)], dtlr[:, bass.ts(q // NH, GW)],
                         start=True, stop=True).then_inc(dtx_ready, 1)
            pe.wait_ge(bc_split, NG)
            pe.wait_ge(dtx_used, NG * NH)
            pe.sem_inc(bc_ready, AHEAD)
            pe.sem_inc(y_added, AHEAD)
            with pe.Fori(0, NG) as c:
                def spread(n):
                    m = c * NS + n
                    pe.wait_ge(read_done, m + 1)
                    t.matmul(bank[:, n % 2, :], sel[:, n, :], bc_hi[:, bass.ts(c, GW)], start=True, stop=True)
                    t.matmul(bank[:, 2 + n % 2, :], sel[:, NS + n, :], bc_hi[:, bass.ts(c, GW)], start=True, stop=True)\
                        .then_inc(bc_ready, 1)
                spread(0)
                spread(1)
                for n in range(NS):
                    m = c * NS + n
                    pe.wait_ge(read_done, m + 1 + AHEAD)
                    if n == 0:
                        pe.wait_ge(y_used, c + 1)
                    for h in range(NH):
                        ins = t.matmul(bank[:, 4 + h, :], ident[:], read[:, n % 2, bass.ts(h, GW)],
                                       start=(n == 0), stop=(n == NS - 1))
                    ins.then_inc(y_added, 1)
                    if n + 2 < NS:
                        spread(n + 2)
                pe.wait_ge(yg_ready, c + 1)
                for i in range(GT):
                    for h in range(NH):
                        ins = t.matmul(bank[:, 6, bass.ts(i, P)], yg[:, h, bass.ts(i, P)], w_out[:, h, :],
                                       start=(h == 0), stop=(h == NH - 1))
                ins.then_inc(proj_ready, 1)
            ffn(1)

        @block.vector
        def _(dve):
            v = nc.vector
            count = [0]

            def settle(ins):
                count[0] += 1
                ins.then_inc(dve_step, 1)
                dve.wait_ge(dve_step, count[0])

            def layer_norm(k, src, dst):
                for j in range(NT):
                    ins = v.bn_stats(stats[:, j, :], src[:, j, :])
                settle(ins)
                for j in range(NT):
                    ins = v.bn_aggr(mv[:, j, :], stats[:, j, :])
                ins.then_inc(var_ready, 1)
                dve.wait_ge(std_ready, k + 1)
                settle(v.reciprocal(rstd[:], std[:]))
                for j in range(NT):
                    ins = v.tensor_scalar(dst[:, j, :], src[:, j, :], mv[:, j, 0:1], rstd[:, j:j + 1],
                                          ALU.subtract, ALU.mult)
                    if k in TURN and j % GT == GT - 1:
                        ins.then_inc(normed_ready, 1)
                if k not in TURN:
                    settle(ins)

            def ffn(r):
                base = STEPS * r
                k0, k1, k2 = FFN_LN[r]
                layer_norm(k0, x, x0)
                layer_norm(k1, x0, normed)
                for g in range(NG):
                    dve.wait_ge(attn_ready, NG * r + g + 1)
                    ins = v.tensor_tensor(hid[:, GT * g:GT * (g + 1), :],
                                          bank[:, 2 + g % 2, :].rearrange("p (t d) -> p t d", d=D),
                                          x0[:, GT * g:GT * (g + 1), :], ALU.add)
                    ins.then_inc(attn_used, 1)
                dve.wait_ge(attn_used, NG * (r + 1))
                layer_norm(k2, hid, normed)
                dve.wait_ge(logits_ready, r + 1)
                settle(v.tensor_copy(logits[:].rearrange("p t e -> p (t e)"), bank[:, 7, 0:NT * NE]))
                for j in range(NT):
                    ins = v.max(top[:, j, :], logits[:, j, :])
                settle(ins)
                v.tensor_tensor(gap[:], top[:, :, 1], top[:, :, 0], ALU.subtract).then_inc(gap_ready, 1)
                for j in range(NT):
                    ins = v.max_index(topi[:, j, :], top[:, j, :], logits[:, j, :])
                settle(ins)
                settle(v.tensor_copy(topf[:], topi[:, :, 0:2]))
                dve.wait_ge(ew_ready, r + 1)
                settle(v.tensor_scalar(w[:, 1, :], ew[:], 1.0, None, ALU.add))
                settle(v.reciprocal(w[:, 0, :], w[:, 1, :]))
                settle(v.tensor_tensor(w[:, 1, :], w[:, 0, :], ew[:], ALU.mult))
                full = [P, NT, NE]
                for k, dst in ((0, comb), (1, pick)):
                    settle(v.tensor_tensor(dst[:], iota8[:].unsqueeze(1).to_broadcast(full),
                                           topf[:, :, k:k + 1].to_broadcast(full), ALU.is_equal))
                    settle(v.tensor_tensor(dst[:], dst[:], w[:, k, :].unsqueeze(2).to_broadcast(full), ALU.mult))
                settle(v.tensor_tensor(comb[:], comb[:], pick[:], ALU.add))

                def mul(n, p):
                    dve.wait_ge(silu_done, n + 1 + AHEAD)
                    dve.wait_ge(turn_done, n + 1)
                    v.tensor_tensor(act[:, p, :], bank[:, 2 + p, :], sg[:, p, :], ALU.mult).then_inc(mul_done, 1)

                def acc(n, p, j, e):
                    dve.wait_ge(down_done, n + 1 + AHEAD)
                    dve.wait_ge(acc_done, n + AHEAD)
                    v.scalar_tensor_tensor(out=hid[:, j, :], in0=bank[:, 6 + p, 0:D], scalar=comb[:, j, e:e + 1],
                                           in1=hid[:, j, :], op0=ALU.mult, op1=ALU.add).then_inc(acc_done, 1)

                for k in range(NE):
                    mul(base + k, k % 2)
                    if k >= 2:
                        acc(base + k - 2, k % 2, 0, k - 2)
                with dve.Fori(1, NT) as j:
                    jm = j - 1
                    for k in range(NE):
                        mul(j * NE + (base + k), k % 2)
                        acc(j * NE + (base + k - 2), k % 2, j if k >= 2 else jm, (k - 2) % NE)
                for k in range(NE, NE + 2):
                    acc(base + STEPS - NE + k - 2, k % 2, NT - 1, k - 2)
                dve.wait_ge(acc_done, base + STEPS + AHEAD)
                settle(v.scalar_tensor_tensor(out=x[:], in0=hid[:], scalar=0.5, in1=x[:], op0=ALU.mult, op1=ALU.add))
                dve.sem_inc(x_ready, 1)

            dve.wait_ge(x_in, 16)
            dve.wait_ge(consts, 5)
            dve.sem_inc(mul_done, AHEAD)
            dve.sem_inc(acc_done, AHEAD)
            ffn(0)

            layer_norm(MAMBA_LN, x, normed)
            dve.wait_ge(mamba_in, MAMBA_LOADS)
            dve.wait_ge(uz_used, NG)
            for h in range(NH):
                for k in range(KC - 1):
                    ins = v.scalar_tensor_tensor(out=u[:, h, :, :], in0=u_raw[:, h, :, k:k + L], scalar=conv_w[:, h, k:k + 1],
                                                 in1=u[:, h, :, :], op0=ALU.mult, op1=ALU.add)
                    if k < KC - 2:
                        settle(ins)
                ins.then_inc(conv_done, 1)
            for g in range(NG):
                hi = bc_hi[:, bass.ts(g, GW)]
                src = bank[0:96, 2 + g % 2, :]
                dve.wait_ge(bcx_ready, g + 1)
                settle(v.tensor_copy(hi, src))
                settle(v.tensor_tensor(bc_r1, src, hi, ALU.subtract))
                settle(v.tensor_copy(bc_mid[:], bc_r1))
                settle(v.tensor_tensor(bc_r2, bc_r1, bc_mid[:], ALU.subtract))
                v.tensor_copy(hi[32:64, :], bc_mid[32:64, :])
                v.tensor_copy(hi[64:96, :], bc_r2[64:96, :]).then_inc(bc_split, 1)
            dve.wait_ge(dt_ready, NG * NH)
            dve.sem_inc(scan_done, AHEAD)
            dve.sem_inc(read_done, AHEAD)
            dve.sem_inc(y_used, 1)
            wide = [P, NH, GW]
            with dve.Fori(0, NG) as c:
                def drive_of(n):
                    m = c * NS + n
                    dve.wait_ge(bc_ready, m + 1 + AHEAD)
                    v.tensor_tensor(drive[:, n % 2, :].rearrange("p (h t) -> p h t", h=NH), dtu[:, :, bass.ts(c, GW)],
                                    bank[:, n % 2, :].unsqueeze(1).to_broadcast(wide), ALU.mult).then_inc(drive_done, 1)
                drive_of(0)
                for n in range(NS):
                    m = c * NS + n
                    dve.wait_ge(decay_ready, m + 1 + AHEAD)
                    dve.wait_ge(drive_done, m + 1)
                    v.tensor_tensor_scan(out=state[:, n % 2, :], data0=decay[:, n % 2, :], data1=drive[:, n % 2, :],
                                         initial=0.0, op0=ALU.mult, op1=ALU.add).then_inc(scan_done, 1)
                    if n + 1 < NS:
                        drive_of(n + 1)
                    dve.wait_ge(scan_done, m + 1 + AHEAD)
                    dve.wait_ge(y_added, m + 1)
                    v.tensor_tensor(read[:, n % 2, :].rearrange("p (h t) -> p h t", h=NH),
                                    state[:, n % 2, :].rearrange("p (h t) -> p h t", h=NH),
                                    bank[:, 2 + n % 2, :].unsqueeze(1).to_broadcast(wide), ALU.mult).then_inc(read_done, 1)
                dve.wait_ge(y_added, c * NS + (NS + AHEAD))
                for h in range(NH):
                    uc = u[:, h, bass.ts(c, GB), :].rearrange("p b l -> p (b l)")
                    ins = v.scalar_tensor_tensor(out=yg[:, h, :], in0=uc, scalar=cols[:, 1, h:h + 1],
                                                 in1=bank[:, 4 + h, :], op0=ALU.mult, op1=ALU.add)
                ins.then_inc(y_used, 1)
                dve.wait_ge(y_used, c + 2)
                v.tensor_tensor(yg, yg, zs[:, :, bass.ts(c, GW)], ALU.mult).then_inc(yg_ready, 1)
                dve.wait_ge(proj_ready, c + 1)
                xc = x[:, bass.ts(c, GT), :].rearrange("p t d -> p (t d)")
                v.tensor_tensor(xc, bank[:, 6, :], xc, ALU.add).then_inc(x_added, 1)
            dve.wait_ge(x_added, NG)
            dve.sem_inc(x_ready, 1)
            ffn(1)


def kernel(**inputs):
    import numpy as np
    import concourse.bacc as bacc
    from concourse.bass_utils import run_bass_kernel_spmd

    def of(name):
        return np.asarray(inputs["L0_" + name])

    wx = of("attn_W_x").reshape(NH, P, DR + 2 * NS).transpose(1, 0, 2)
    arrays = {
        "x": of("attn_x").reshape(NT * P, D),
        "ln_cols": np.stack([of("ffn_ln1_g"), of("ffn_ln1_b"), of("ffn_ln2_g"), of("ffn_ln2_b")], axis=1),
        "attn_w": of("ffn_attn_w").T,
        "router_w": of("ffn_gate_w").T,
        "gate_w": of("ffn_gate_proj").transpose(2, 0, 1),
        "up_w": of("ffn_up_proj").transpose(2, 0, 1),
        "down_w": of("ffn_down_proj").reshape(NE, D, NI, P).transpose(3, 0, 2, 1),
        "w_in": of("attn_W_in"),
        "conv_w": of("attn_conv_w").reshape(NH, P, KC).transpose(1, 0, 2),
        "cols": np.stack([of("attn_conv_b"), of("attn_D"), of("attn_b_dt")]).reshape(3, NH, P).transpose(2, 0, 1),
        "w_dtlr": wx[:, :, 0:DR],
        "w_bc": np.concatenate([wx[:, :, DR:]] * 3, axis=2),
        "w_dt": of("attn_W_dt"),
        "w_out": of("attn_W_out").reshape(NH, P, D).transpose(1, 0, 2),
        "A_log": of("attn_A_log"),
    }
    arrays = {"in_" + k: np.ascontiguousarray(v) for k, v in arrays.items()}
    nc = bacc.Bacc("TRN2", target_bir_lowering=False, num_devices=1)
    aps = {k[3:]: nc.dram_tensor(k, v.shape, mybir.dt.from_np(v.dtype), kind="ExternalInput").ap()
           for k, v in arrays.items()}
    out = nc.dram_tensor("out", (NT * P, D), F32, kind="ExternalOutput").ap()
    macaron(nc, aps, out)
    r = run_bass_kernel_spmd(nc, [arrays], core_ids=[0])
    return r.results[0]["out"].reshape(NB, L, D)
```

```python
from contextlib import ExitStack

import concourse.bass as bass
from concourse import mybir

ALU = mybir.AluOpType
ACT = mybir.ActivationFunctionType
F32 = mybir.dt.float32
BF16 = mybir.dt.bfloat16
U32 = mybir.dt.uint32

P = 128
D = 128
NT = 16
GT = 4
NG = NT // GT
GW = GT * P
NE = 8
FI = 512
NI = FI // P
DI = 256
NH = DI // P
NB = 8
L = 256
GB = GW // L
NS = 16
DR = 64
KC = 4
EPS = 1e-5
TOPK = 2
NA = TOPK * NT
RING = 4
STEPS = -(-((TOPK * NT * P - NE) // P + NE) // RING) * RING
NOWHERE = TOPK * NT * P
AHEAD = 2


def macaron(nc, a, out):
    ctx = ExitStack()
    with ctx:
        def sb(name, shape, dt=F32):
            return ctx.enter_context(nc.sbuf_tensor(name, shape, dt))

        def sem(name):
            return ctx.enter_context(nc.semaphore(name))

        bank = ctx.enter_context(nc.psum_tensor("bank", [P, 8, 512], F32))
        x = sb("x", [P, NT, D])
        normed = sb("normed", [P, NT, D])
        x0 = sb("x0", [P, NT, D])
        hid = sb("hid", [P, NT, D])
        aT = sb("aT", [P, NT * P])
        tT = sb("tT", [P, NT * P])
        gate_w = sb("gate_w", [P, NE, FI])
        up_w = sb("up_w", [P, NE, FI])
        down_w = sb("down_w", [P, NE, NI, D])
        attn_w = sb("attn_w", [P, D])
        router_w = sb("router_w", [P, NE])
        ln_cols = sb("ln_cols", [P, 4])
        ident = sb("ident", [P, P])
        iota8 = sb("iota8", [P, NE])
        eps = sb("eps", [P, 1])
        stats = sb("stats", [P, NT, 6])
        mv = sb("mv", [P, NT, 2])
        std = sb("std", [P, NT])
        rstd = sb("rstd", [P, NT])
        logits = sb("logits", [P, NT, NE])
        top = sb("top", [P, NT, 8])
        topi = sb("topi", [P, NT, 8], U32)
        topf = sb("topf", [P, NT, 2])
        gap = sb("gap", [P, NT])
        ew = sb("ew", [P, NT])
        w = sb("w", [P, 2, NT])
        rows = sb("rows", [P, RING, D])
        tile = sb("tile", [P, 2, P])
        y_row = sb("y_row", [P, RING, D])
        upper = sb("upper", [P, P])
        ones = sb("ones", [P, P])
        iota_lane = sb("iota_lane", [P, P])
        lane = sb("lane", [P, 1])
        hot = sb("hot", [P, TOPK, NT, NE])
        both = sb("both", [P, NT, NE])
        tot = sb("tot", [P, NE, NT])
        incl = sb("incl", [P, NE, NT])
        keep = sb("keep", [P, NE, NT])
        over = sb("over", [P, NE, NT])
        e_tiles = sb("e_tiles", [P, NE])
        e_end = sb("e_end", [P, NE])
        e_base = sb("e_base", [P, NE])
        slot = sb("slot", [P, NA])
        slot_i = sb("slot_i", [P, 3, NA], U32)
        slot_f = sb("slot_f", [P, 2, NA])
        found = sb("found", [P, 3, STEPS])
        dest_f = sb("dest_f", [P, STEPS])
        dest = sb("dest", [P, STEPS], U32)
        source = sb("source", [P, STEPS], U32)
        dest_now = sb("dest_now", [P, RING], U32)
        source_now = sb("source_now", [P, RING], U32)
        past = sb("past", [P, STEPS, NE])
        expert_f = sb("expert_f", [P, STEPS])
        expert = sb("expert", [P, STEPS], mybir.dt.int32)
        sg = sb("sg", [P, 2, FI])
        act = sb("act", [P, 2, FI])
        actT = sb("actT", [P, 2, FI])
        w_in = sb("w_in", [P, 2 * DI])
        conv_w = sb("conv_w", [P, NH, KC])
        cols = sb("cols", [P, 3, NH])
        w_dtlr = sb("w_dtlr", [P, NH, DR])
        w_bc = sb("w_bc", [P, NH, 3 * 2 * NS])
        w_dt = sb("w_dt", [DR, DI])
        w_out = sb("w_out", [P, NH, D])
        a_col = sb("a_col", [P, NS])
        u_raw = sb("u_raw", [P, NH, NB, L + KC - 1])
        dt = u_raw[:].rearrange("p h b l -> p (h b l)")[:, 0:NH * NB * L].rearrange("p (h b l) -> p h b l", h=NH, b=NB)
        u = sb("u", [P, NH, NB, L])
        zs = sb("zs", [P, NH, NT * P])
        dtu = sb("dtu", [P, NH, NT * P])
        dtlr = tT[0:DR, :]
        hots = dtu[:].rearrange("p h n -> p (h n)").bitcast(BF16)
        low_hot = hots[:, 0:NA * P].rearrange("p (c n) -> p c n", c=NA)
        high_hot = hots[:, NA * P:NA * (P + 3 * STEPS)].rearrange("p (c a n) -> p c a n", c=NA, a=3)
        bc_hi = sb("bc_hi", [96, NT * P], BF16)
        bc_mid = sb("bc_mid", [96, GW], BF16)
        bc_r1, bc_r2 = actT[0:96, 0, :], actT[0:96, 1, :]
        sel = sb("sel", [96, 2 * NS, P], BF16)

        def scan_buffer(t):
            return t[:].rearrange("p a b -> p (a b)").rearrange("p (s n) -> p s n", s=2)
        b_row = normed[:].rearrange("p t d -> p (t d)")[:, 0:2 * GW].rearrange("p (s n) -> p s n", s=2)
        drive = scan_buffer(x0)
        state = scan_buffer(hid)
        read = tT[:].rearrange("p (s n) -> p s n", s=2)
        sp_exp = [dtu[:, :, bass.ts(g, GW)] for g in range(NG)]
        sp_relu = [dt[:, :, GB * g:GB * (g + 1), :].rearrange("p h b l -> p h (b l)") for g in range(NG)]
        sp_ln = [(state, drive)[g // 2][:, g % 2, :].rearrange("p (h n) -> p h n", h=NH) for g in range(NG)]
        sp_tmp = [sg, act]
        yg = aT[:, 0:NH * GW].rearrange("p (s n) -> p s n", s=NH)
        decay = [bank[:, 2 * i:2 * i + 2, :] for i in range(2)]

        t_rows = nc.dram_tensor("t_rows", [NT * P, D], F32, kind="Internal").ap()
        y_rows = nc.dram_tensor("y_rows", [TOPK * NT * P, D], F32, kind="Internal").ap()

        t_out = sem("t_out")
        gathered = [sem(f"gathered{b}") for b in range(RING)]
        y_sent = [sem(f"y_sent{b}") for b in range(RING)]
        y_back = [sem(f"y_back{g}") for g in range(NG)]
        both_ready = sem("both_ready"); ranks_ready = sem("ranks_ready"); hot_ready = sem("hot_ready")
        found_ready = sem("found_ready"); plan_ready = sem("plan_ready")
        in_turned = sem("in_turned"); in_taken = sem("in_taken"); y_taken = sem("y_taken")
        x_in = sem("x_in"); small_in = sem("small_in"); big_in = sem("big_in"); mamba_in = sem("mamba_in")
        out_sent = sem("out_sent")
        consts = sem("consts"); pool_step = sem("pool_step")
        dve_step = sem("dve_step"); act_step = sem("act_step")
        var_ready = sem("var_ready"); std_ready = sem("std_ready"); normed_ready = sem("normed_ready")
        turned = sem("turned"); turned_used = sem("turned_used")
        attn_ready = sem("attn_ready"); attn_used = sem("attn_used")
        logits_ready = sem("logits_ready"); gap_ready = sem("gap_ready"); ew_ready = sem("ew_ready")
        gu_ready = sem("gu_ready"); silu_done = sem("silu_done")
        mul_done = sem("mul_done"); turn_done = sem("turn_done"); evac_done = sem("evac_done")
        down_done = sem("down_done")
        x_ready = sem("x_ready")
        uz_ready = sem("uz_ready"); uz_used = sem("uz_used")
        conv_done = sem("conv_done"); u_ready = sem("u_ready")
        bcx_ready = sem("bcx_ready"); bc_split = sem("bc_split"); dtlr_ready = sem("dtlr_ready")
        dtx_ready = sem("dtx_ready"); dtx_used = sem("dtx_used"); sp_ready = sem("sp_ready"); x_added = sem("x_added")
        dt_ready = sem("dt_ready"); wait_carrier = sem("wait_carrier"); row_free = sem("row_free"); zero_ready = sem("zero_ready"); index_ready = sem("index_ready"); decay_begun = sem("decay_begun")
        b_spread = sem("b_spread"); c_spread = sem("c_spread"); b_copied = sem("b_copied"); dtu_ready = sem("dtu_ready"); decay_ready = sem("decay_ready"); drive_done = sem("drive_done")
        scan_done = sem("scan_done"); read_done = sem("read_done"); y_added = sem("y_added")
        yg_ready = sem("yg_ready"); y_used = sem("y_used"); proj_ready = sem("proj_ready")

        block = ctx.enter_context(nc.Block())

        LN_RUNS = 2 + 2 + 1 + 2
        FFN_LN = [[0, 1, 2], [4, 5, 6]]
        MAMBA_LN = 3
        TURN = {1: 0, 2: 1, 3: 2, 5: 3, 6: 4}

        @block.sync
        def _(sp):
            sp.dma_start(x[:], a["x"].rearrange("(t p) d -> p t d", p=P)).then_inc(x_in, 16)
            sp.dma_start(ln_cols[:], a["ln_cols"]).then_inc(small_in, 16)
            sp.dma_start(attn_w[:], a["attn_w"]).then_inc(small_in, 16)
            sp.dma_start(router_w[:], a["router_w"]).then_inc(small_in, 16)
            sp.dma_start(gate_w[:], a["gate_w"]).then_inc(big_in, 16)
            sp.dma_start(up_w[:], a["up_w"]).then_inc(big_in, 16)
            sp.dma_start(down_w[:], a["down_w"]).then_inc(big_in, 16)
            sp.dma_start(w_in[:], a["w_in"]).then_inc(mamba_in, 16)
            sp.dma_start(conv_w[:], a["conv_w"]).then_inc(mamba_in, 16)
            sp.dma_start(cols[:], a["cols"]).then_inc(mamba_in, 16)
            sp.dma_start(w_dtlr[:], a["w_dtlr"]).then_inc(mamba_in, 16)
            sp.dma_start(w_bc[:], a["w_bc"]).then_inc(mamba_in, 16)
            sp.dma_start(w_dt[:], a["w_dt"]).then_inc(mamba_in, 16)
            sp.dma_start(w_out[:], a["w_out"]).then_inc(mamba_in, 16)
            sp.dma_start(a_col[:], a["A_log"].partition_broadcast(P)).then_inc(mamba_in, 16)
            for r in range(2):
                sp.wait_ge(normed_ready, NG * (TURN[FFN_LN[r][2]] + 1))
                sp.dma_start(t_rows.rearrange("(t p) d -> p t d", p=P), normed[:]).then_inc(t_out, 16)
                for b in range(RING):
                    sp.wait_ge(y_sent[b], 16 * (r + 1) * STEPS // RING)
                y_view = y_rows.rearrange("(k g t p) d -> g k p t d", k=TOPK, g=NG, p=P)
                for g in range(NG):
                    for k, dst in ((0, normed), (1, x0)):
                        sp.dma_start(dst[:, GT * g:GT * (g + 1), :], y_view[g, k]).then_inc(y_back[g], 16)
            sp.wait_ge(x_ready, 3)
            sp.dma_start(out.rearrange("(t p) d -> p t d", p=P), x[:]).then_inc(out_sent, 16)
            sp.wait_ge(out_sent, 16)
        MAMBA_LOADS = 16 * 8
        CONSTS = 9
        SEL = 7

        @block.gpsimd
        def _(pool):
            g = nc.gpsimd
            g.memset(ident[:], 0.0).then_inc(pool_step, 1)
            g.memset(eps[:], EPS).then_inc(consts, 1)
            g.iota(iota8[:], [[1, NE]], base=0, channel_multiplier=0, allow_small_or_imprecise_dtypes=True).then_inc(consts, 1)
            g.memset(u_raw[:, :, :, 0:KC - 1], 0.0).then_inc(consts, 1)
            g.memset(ones[:], 1.0).then_inc(consts, 1)
            g.memset(upper[:], 1.0).then_inc(pool_step, 1)
            g.memset(keep[:], 1.0).then_inc(pool_step, 1)
            g.iota(iota_lane[:], [[1, P]], base=0, channel_multiplier=0, allow_small_or_imprecise_dtypes=True).then_inc(consts, 1)
            g.iota(lane[:], [[0, 1]], base=0, channel_multiplier=1, allow_small_or_imprecise_dtypes=True).then_inc(consts, 1)
            pool.wait_ge(pool_step, 3)
            g.memset(keep[:, :, 0:1], 0.0).then_inc(consts, 1)
            g.affine_select(out=upper[:], in_=upper[:], compare_op=ALU.is_gt, fill=0.0, base=0,
                            pattern=[[1, P]], channel_multiplier=-1).then_inc(consts, 1)
            g.affine_select(out=ident[:], in_=ident[:], compare_op=ALU.not_equal, fill=1.0, base=0,
                            pattern=[[-1, P]], channel_multiplier=1).then_inc(consts, 1)
            g.memset(sel[:], 0.0).then_inc(pool_step, 1)
            for part in range(3):
                pool.wait_ge(pool_step, 4 + part)
                g.affine_select(out=sel[:], in_=sel[:], compare_op=ALU.not_equal, fill=1.0, base=-32 * part,
                                pattern=[[-1, 2 * NS], [0, P]], channel_multiplier=1).then_inc(pool_step, 1)

            def gather_and_scatter(r):
                base = STEPS * r

                def gather(b):
                    g.indirect_dma_start(out=rows[:, b, :], out_offset=None, in_=t_rows,
                                         in_offset=bass.IndirectOffsetOnAxis(ap=source_now[:, b:b + 1], axis=0),
                                         bounds_check=NT * P - 1, oob_is_err=False).then_inc(gathered[b], 16)

                def scatter(n, b):
                    pool.wait_ge(y_taken, n + (base + 2))
                    pool.sem_inc(wait_carrier, 1)
                    g.indirect_dma_start(out=y_rows, out_offset=bass.IndirectOffsetOnAxis(ap=dest_now[:, b:b + 1], axis=0),
                                         in_=y_row[:, b, :], in_offset=None,
                                         bounds_check=NOWHERE - 1, oob_is_err=False).then_inc(y_sent[b], 16)

                def index(of, now, n, b):
                    g.tensor_copy(now[:, b:b + 1], of[:, bass.ds(n, 1)]).then_inc(index_ready, 1)

                pool.wait_ge(plan_ready, r + 1)
                pool.wait_ge(t_out, 16 * (r + 1))
                t0 = 16 * (base // RING)
                for b in range(RING):
                    index(source, source_now, b, b)
                    pool.wait_ge(index_ready, 2 * base + b + 1)
                    gather(b)
                def turn(q, gather_more=True):
                    for b in range(RING):
                        n = q * RING + b
                        if gather_more:
                            pool.wait_ge(gathered[b], q * 16 + (t0 + 16))
                            index(source, source_now, n + RING, b)
                        if not (r == 0 and isinstance(q, int) and q == 0):
                            pool.wait_ge(y_sent[b], q * 16 + t0)
                        pool.sem_inc(row_free, 1)
                        index(dest, dest_now, n, b)
                        if gather_more:
                            pool.wait_ge(index_ready, n * 2 + (2 * base + RING + 2))
                            pool.wait_ge(in_turned, n + (base + 1))
                            pool.sem_inc(wait_carrier, 1)
                            gather(b)
                        else:
                            pool.wait_ge(index_ready, n + (2 * base + STEPS + 1))
                        scatter(n, b)

                turn(0)
                with pool.Fori(1, STEPS // RING - 1) as q:
                    turn(q)
                turn(STEPS // RING - 1, gather_more=False)

            gather_and_scatter(0)
            for gq in range(NG):
                pool.wait_ge(dt_ready, gq + 1)
                g.tensor_tensor(dtu[:, :, bass.ts(gq, GW)], dt[:, :, GB * gq:GB * (gq + 1), :].rearrange("p h b l -> p h (b l)"),
                                u[:, :, GB * gq:GB * (gq + 1), :].rearrange("p h b l -> p h (b l)"), ALU.mult)\
                    .then_inc(dtu_ready, 1)
            pool.wait_ge(dtu_ready, NG)
            with pool.Fori(0, NG) as c:
                for n in range(NS):
                    m = c * NS + n
                    pool.wait_ge(b_copied, m + 1 + 1)
                    pool.wait_ge(scan_done, m + 1)
                    pool.sem_inc(wait_carrier, 1)
                    g.tensor_tensor(drive[:, n % 2, :].rearrange("p (h t) -> p h t", h=NH), dtu[:, :, bass.ts(c, GW)],
                                    b_row[:, n % 2, :].unsqueeze(1).to_broadcast([P, NH, GW]), ALU.mult).then_inc(drive_done, 1)
            gather_and_scatter(1)

        @block.scalar
        def _(eng):
            s = nc.scalar

            def std_of(k):
                eng.wait_ge(var_ready, k + 1)
                s.activation(std[:], mv[:, :, 1], ACT.Sqrt, bias=eps[:, 0:1]).then_inc(std_ready, 1)

            def turned_out(k, dst, scale, bias):
                for g in range(NG):
                    n = NG * TURN[k] + g
                    eng.wait_ge(turned, n + 1)
                    s.activation(dst[:, bass.ts(g, GW)], bank[:, n % 2, :], ACT.Identity, bias=bias, scale=scale)\
                        .then_inc(turned_used, 1)

            def ffn(r):
                base = STEPS * r
                std_of(FFN_LN[r][0])
                std_of(FFN_LN[r][1])
                turned_out(FFN_LN[r][1], aT, ln_cols[:, 0:1], ln_cols[:, 1:2])
                std_of(FFN_LN[r][2])
                turned_out(FFN_LN[r][2], tT, ln_cols[:, 2:3], ln_cols[:, 3:4])
                eng.wait_ge(gap_ready, r + 1)
                s.activation(ew[:], gap[:], ACT.Exp).then_inc(ew_ready, 1)

                def silu(n, p):
                    eng.wait_ge(gu_ready, n + 1)
                    eng.wait_ge(mul_done, n + 1)
                    s.activation(sg[:, p, :], bank[:, p, :], ACT.Silu).then_inc(silu_done, 1)

                def evac(n, p):
                    eng.wait_ge(turn_done, n + 1 + AHEAD)
                    eng.wait_ge(down_done, n + 1)
                    s.activation(actT[:, p, :], bank[:, 4 + p, :], ACT.Copy).then_inc(evac_done, 1)

                def take_in(n, p):
                    eng.wait_ge(in_turned, n + 1)
                    s.activation(tile[:, p, :], bank[:, 7, 0:P], ACT.Identity, bias=ln_cols[:, 3:4], scale=ln_cols[:, 2:3])\
                        .then_inc(in_taken, 1)

                def step(n, k, ahead=2):
                    if ahead > 0:
                        silu(n + 1, (k + 1) % 2)
                    if ahead > 1:
                        take_in(n + 2, k % 2)
                    evac(n, k % 2)

                take_in(base, 0)
                take_in(base + 1, 1)
                silu(base, 0)
                step(base, 0)
                with eng.Fori(0, STEPS // RING - 1) as q:
                    for k in range(1, RING + 1):
                        step(q * RING + (base + k), k)
                for k in range(1, RING):
                    step(base + STEPS - RING + k, k, RING - 1 - k)

            eng.wait_ge(consts, CONSTS)
            eng.wait_ge(small_in, 16 * 3)
            eng.sem_inc(silu_done, AHEAD)
            eng.sem_inc(evac_done, AHEAD)
            eng.sem_inc(in_taken, 1)
            ffn(0)

            std_of(MAMBA_LN)
            turned_out(MAMBA_LN, aT, 1.0, 0.0)
            eng.wait_ge(mamba_in, MAMBA_LOADS)
            for g in range(NG):
                eng.wait_ge(uz_ready, g + 1)
                for h in range(NH):
                    s.activation(u_raw[:, h, GB * g:GB * (g + 1), KC - 1:],
                                 bank[:, 4 + h, :].rearrange("p (b l) -> p b l", l=L), ACT.Copy)
                    s.activation(u[:, h, GB * g:GB * (g + 1), :].rearrange("p b l -> p (b l)"), bank[:, 4 + h, :],
                                 ACT.Identity, bias=cols[:, 0, h:h + 1], scale=conv_w[:, h, KC - 1:KC])
                for h in range(NH):
                    ins = s.activation(zs[:, h, bass.ts(g, GW)], bank[:, 6 + h, :], ACT.Silu)
                ins.then_inc(uz_used, 1)
            for h in range(NH):
                eng.wait_ge(conv_done, h + 1)
                uh = u[:, h, :, :].rearrange("p b l -> p (b l)")
                s.activation(uh, uh, ACT.Silu).then_inc(u_ready, 1)
            s.activation(a_col[:], a_col[:], ACT.Exp).then_inc(act_step, 1)
            eng.wait_ge(act_step, 1)
            s.activation(a_col[:], a_col[:], ACT.Copy, scale=-1.0).then_inc(act_step, 1)
            for g in range(NG):
                eng.wait_ge(bcx_ready, g + 1)
                s.activation(dtlr[:, bass.ts(g, GW)], bank[0:DR, g % 2, :], ACT.Copy).then_inc(dtlr_ready, 1)
            for g in range(NG):
                p = g % 2
                eng.wait_ge(dtx_ready, g + 1)
                for h in range(NH):
                    s.activation(sp_exp[g][:, h, :], bank[:, 4 + 2 * p + h, :], ACT.Abs, bias=cols[:, 2, h:h + 1])
                for h in range(NH):
                    ins = s.activation(sp_relu[g][:, h, :], bank[:, 4 + 2 * p + h, :], ACT.Relu, bias=cols[:, 2, h:h + 1])
                ins.then_inc(dtx_used, 1)
                eng.wait_ge(dtx_used, g + 1)
                s.activation(sp_exp[g], sp_exp[g], ACT.Exp, scale=-1.0).then_inc(act_step, 1)
            for g in range(NG):
                eng.wait_ge(act_step, 2 + g + 1)
                s.activation(sp_ln[g], sp_exp[g], ACT.Ln, bias=1.0).then_inc(sp_ready, 1)
            eng.wait_ge(zero_ready, 1)
            eng.sem_inc(decay_ready, AHEAD)
            eng.sem_inc(b_copied, 1)
            s.preload_act_table(ACT.Exp)
            with eng.Fori(0, NG) as c:
                for n in range(NS):
                    m = c * NS + n
                    eng.wait_ge(b_spread, m + 1)
                    eng.wait_ge(drive_done, m + 1)
                    s.activation(b_row[:, n % 2, :], bank[:, 6, :], ACT.Copy).then_inc(b_copied, 1)
                    eng.wait_ge(scan_done, m + 1)
                    eng.sem_inc(decay_begun, 1)
                    out_v = decay[n % 2].rearrange("p h (b l) -> p h b l", l=L)
                    s.activation(out_v[:, :, :, 1:L], dt[:, :, bass.ts(c, GB), 1:L],
                                 ACT.Exp, scale=a_col[:, n:n + 1]).then_inc(decay_ready, 1)
            ffn(1)

        @block.tensor
        def _(pe):
            t = nc.tensor

            def turn_group(k, g):
                n = NG * TURN[k] + g
                pe.wait_ge(normed_ready, n + 1)
                if n >= 2:
                    pe.wait_ge(turned_used, n - 1)
                for i in range(GT):
                    ins = t.transpose(bank[:, n % 2, bass.ts(i, P)], normed[:, GT * g + i, :], ident[:])
                ins.then_inc(turned, 1)

            def ffn(r):
                base = STEPS * r
                k1, k2 = FFN_LN[r][1:]
                for g in range(NG):
                    turn_group(k1, g)
                    n = NG * r + g
                    pe.wait_ge(turned_used, NG * TURN[k1] + g + 1)
                    if n >= 2:
                        pe.wait_ge(attn_used, n - 1)
                    for i in range(GT):
                        ins = t.matmul(bank[:, 2 + g % 2, bass.ts(i, P)], aT[:, bass.ts(GT * g + i, P)], attn_w[:],
                                       start=True, stop=True)
                    ins.then_inc(attn_ready, 1)
                for g in range(NG):
                    turn_group(k2, g)
                    pe.wait_ge(turned_used, NG * TURN[k2] + g + 1)
                    for i in range(GT):
                        j = GT * g + i
                        ins = t.matmul(bank[:, 7, bass.ts(j, NE)], tT[:, bass.ts(j, P)], router_w[:],
                                       start=True, stop=True)
                ins.then_inc(logits_ready, 1)
                pe.wait_ge(both_ready, r + 1)
                pe_flat = both[:].rearrange("p t e -> p (t e)")
                t.matmul(bank[:, 6, 0:NT * NE], upper[:], pe_flat, start=True, stop=True)
                t.matmul(bank[:, 6, 128:128 + NT * NE], ones[:], pe_flat, start=True, stop=True).then_inc(ranks_ready, 1)
                pe.wait_ge(hot_ready, r + 1)
                for c in range(NA):
                    ins = t.matmul(bank[:, 7, 0:3 * STEPS], low_hot[:, c, :],
                                   high_hot[:, c, :, :].rearrange("p a n -> p (a n)"), start=(c == 0), stop=(c == NA - 1))
                ins.then_inc(found_ready, 1)

                def turn_in(n, k, turn):
                    pe.wait_ge(gathered[k % RING], turn)
                    pe.wait_ge(in_taken, n + 1)
                    t.transpose(bank[:, 7, 0:P], rows[:, k % RING, :], ident[:]).then_inc(in_turned, 1)

                def expert_of(m):
                    return pe.value_load(expert[0:1, bass.ds(m, 1)], min_val=0, max_val=NE - 1)

                def gate_up(n, k, e):
                    pe.wait_ge(in_taken, n + 1 + 1)
                    pe.wait_ge(silu_done, n + 1)
                    pe.wait_ge(mul_done, n + 1)
                    t.matmul(bank[:, k % 2, :], tile[:, k % 2, :], gate_w[:, bass.ds(e, 1), :].rearrange("p a n -> p (a n)"),
                             start=True, stop=True)
                    t.matmul(bank[:, 2 + k % 2, :], tile[:, k % 2, :], up_w[:, bass.ds(e, 1), :].rearrange("p a n -> p (a n)"),
                             start=True, stop=True).then_inc(gu_ready, 1)

                def turn(n, p):
                    pe.wait_ge(mul_done, n + 1 + AHEAD)
                    pe.wait_ge(evac_done, n + 1)
                    for i in range(NI):
                        ins = t.transpose(bank[:, 4 + p, bass.ts(i, P)], act[:, p, bass.ts(i, P)], ident[:])
                    ins.then_inc(turn_done, 1)

                def down(n, p, e):
                    pe.wait_ge(evac_done, n + 1 + AHEAD)
                    pe.wait_ge(y_taken, n + 1)
                    for i in range(NI):
                        ins = t.matmul(bank[:, 6, 0:D], actT[:, p, bass.ts(i, P)],
                                       down_w[:, bass.ds(e, 1), i, :].rearrange("p a n -> p (a n)"),
                                       start=(i == 0), stop=(i == NI - 1))
                    ins.then_inc(down_done, 1)

                def steps_of(m0, k0, count, turns, last=False):
                    known = {k0 + i: expert_of(m0 + i) for i in (-1, 0, 1) if m0 is not None and (i >= 0 or k0 > 0) and
                             not (last and count == 0)}
                    for i in range(count):
                        m, k = m0 + i, k0 + i
                        n = m + base
                        ahead = 2 if not last else count - 1 - i
                        if ahead > 0:
                            gate_up(n + 1, k + 1, known[k + 1])
                        if i + 1 < count and ahead > 1:
                            known[k + 2] = expert_of(m + 2)
                        turn(n, k % 2)
                        if ahead > 1:
                            turn_in(n + 2, k + 2, turns((k + 2) // RING))
                        if k > 0:
                            down(n - 1, (k - 1) % 2, known[k - 1])
                    return known

                pe.wait_ge(plan_ready, r + 1)
                pe.wait_ge(big_in, 16 * 3)
                t0 = 16 * (base // RING)
                turn_in(base, 0, t0 + 16)
                turn_in(base + 1, 1, t0 + 16)
                gate_up(base, 0, expert_of(0))
                steps_of(0, 0, 1, lambda d: t0 + 16 * d + 16)
                with pe.Fori(0, STEPS // RING - 1) as q:
                    steps_of(q * RING + 1, 1, RING, lambda d: q * 16 + (t0 + 16 * d + 16))
                known = steps_of(STEPS - RING + 1, STEPS - RING + 1, RING - 1, lambda d: t0 + 16 * d + 16, last=True)
                down(base + STEPS - 1, (STEPS - 1) % 2, known[STEPS - 1])

            pe.wait_ge(consts, CONSTS)
            pe.wait_ge(small_in, 16 * 3)
            pe.sem_inc(turn_done, AHEAD)
            pe.sem_inc(down_done, AHEAD)
            ffn(0)

            for g in range(NG):
                turn_group(MAMBA_LN, g)
            pe.wait_ge(mamba_in, MAMBA_LOADS)
            for g in range(NG):
                pe.wait_ge(turned_used, NG * TURN[MAMBA_LN] + g + 1)
                if g == 0:
                    pe.wait_ge(x_ready, 1)
                else:
                    pe.wait_ge(uz_used, g)
                for q in range(2 * NH):
                    ins = t.matmul(bank[:, 4 + q, :], w_in[:, bass.ts(q, P)], aT[:, bass.ts(g, GW)], start=True, stop=True)
                ins.then_inc(uz_ready, 1)
            pe.wait_ge(u_ready, NH)
            for g in range(NG):
                if g >= 2:
                    pe.wait_ge(dtlr_ready, g - 1)
                    pe.wait_ge(bc_split, g - 1)
                for h in range(NH):
                    t.matmul(bank[0:DR, g % 2, :], w_dtlr[:, h, :], u[:, h, GB * g:GB * (g + 1), :].rearrange("p b l -> p (b l)"),
                             start=(h == 0), stop=(h == NH - 1))
                for h in range(NH):
                    ins = t.matmul(bank[0:96, 2 + g % 2, :], w_bc[:, h, :], u[:, h, GB * g:GB * (g + 1), :].rearrange("p b l -> p (b l)"),
                                   start=(h == 0), stop=(h == NH - 1))
                ins.then_inc(bcx_ready, 1)
            pe.wait_ge(uz_used, NG)
            for g in range(NG):
                pe.wait_ge(dtlr_ready, g + 1)
                if g >= 2:
                    pe.wait_ge(dtx_used, g - 1)
                for h in range(NH):
                    ins = t.matmul(bank[:, 4 + 2 * (g % 2) + h, :], w_dt[:, bass.ts(h, P)], dtlr[:, bass.ts(g, GW)],
                                   start=True, stop=True)
                ins.then_inc(dtx_ready, 1)
            pe.wait_ge(bc_split, NG)
            pe.wait_ge(dtx_used, NG)
            pe.wait_ge(pool_step, SEL)
            pe.sem_inc(y_added, AHEAD)
            with pe.Fori(0, NG) as c:
                def spread_b(n):
                    pe.wait_ge(b_copied, c * NS + (n + 1))
                    t.matmul(bank[:, 6, :], sel[:, n, :], bc_hi[:, bass.ts(c, GW)], start=True, stop=True)\
                        .then_inc(b_spread, 1)

                def spread_c(n):
                    if n == 0:
                        pe.wait_ge(x_added, c + 1)
                    pe.wait_ge(read_done, c * NS + (n + AHEAD))
                    t.matmul(bank[:, 7, :], sel[:, NS + n, :], bc_hi[:, bass.ts(c, GW)], start=True, stop=True)\
                        .then_inc(c_spread, 1)

                def add(n):
                    pe.wait_ge(read_done, c * NS + (n + 1 + AHEAD))
                    if n == 0:
                        pe.wait_ge(y_used, c + 1)
                    for h in range(NH):
                        ins = t.matmul(bank[:, 4 + h, :], ident[:], read[:, n % 2, bass.ts(h, GW)],
                                       start=(n == 0), stop=(n == NS - 1))
                    ins.then_inc(y_added, 1)
                spread_b(0)
                spread_b(1)
                for n in range(NS):
                    spread_c(n)
                    if n + 2 < NS:
                        spread_b(n + 2)
                    if n > 0:
                        add(n - 1)
                add(NS - 1)
                pe.wait_ge(yg_ready, c + 1)
                for i in range(GT):
                    for h in range(NH):
                        ins = t.matmul(bank[:, 7, bass.ts(i, P)], yg[:, h, bass.ts(i, P)], w_out[:, h, :],
                                       start=(h == 0), stop=(h == NH - 1))
                ins.then_inc(proj_ready, 1)
            ffn(1)

        @block.vector
        def _(dve):
            v = nc.vector
            count = [0]

            def settle(ins):
                count[0] += 1
                ins.then_inc(dve_step, 1)
                dve.wait_ge(dve_step, count[0])

            def layer_norm(k, src, dst):
                for j in range(NT):
                    ins = v.bn_stats(stats[:, j, :], src[:, j, :])
                settle(ins)
                for j in range(NT):
                    ins = v.bn_aggr(mv[:, j, :], stats[:, j, :])
                ins.then_inc(var_ready, 1)
                dve.wait_ge(std_ready, k + 1)
                settle(v.reciprocal(rstd[:], std[:]))
                for j in range(NT):
                    ins = v.tensor_scalar(dst[:, j, :], src[:, j, :], mv[:, j, 0:1], rstd[:, j:j + 1],
                                          ALU.subtract, ALU.mult)
                    if k in TURN and j % GT == GT - 1:
                        ins.then_inc(normed_ready, 1)
                if k not in TURN:
                    settle(ins)

            def ffn(r):
                base = STEPS * r
                k0, k1, k2 = FFN_LN[r]
                layer_norm(k0, x, x0)
                layer_norm(k1, x0, normed)
                for g in range(NG):
                    dve.wait_ge(attn_ready, NG * r + g + 1)
                    ins = v.tensor_tensor(hid[:, GT * g:GT * (g + 1), :],
                                          bank[:, 2 + g % 2, :].rearrange("p (t d) -> p t d", d=D),
                                          x0[:, GT * g:GT * (g + 1), :], ALU.add)
                    ins.then_inc(attn_used, 1)
                dve.wait_ge(attn_used, NG * (r + 1))
                layer_norm(k2, hid, normed)
                dve.wait_ge(logits_ready, r + 1)
                settle(v.tensor_copy(logits[:].rearrange("p t e -> p (t e)"), bank[:, 7, 0:NT * NE]))
                for j in range(NT):
                    ins = v.max(top[:, j, :], logits[:, j, :])
                settle(ins)
                v.tensor_tensor(gap[:], top[:, :, 1], top[:, :, 0], ALU.subtract).then_inc(gap_ready, 1)
                for j in range(NT):
                    ins = v.max_index(topi[:, j, :], top[:, j, :], logits[:, j, :])
                settle(ins)
                settle(v.tensor_copy(topf[:], topi[:, :, 0:2]))
                dve.wait_ge(ew_ready, r + 1)
                settle(v.tensor_scalar(w[:, 1, :], ew[:], 1.0, None, ALU.add))
                settle(v.reciprocal(w[:, 0, :], w[:, 1, :]))
                settle(v.tensor_tensor(w[:, 1, :], w[:, 0, :], ew[:], ALU.mult))
                full = [P, NT, NE]
                for k in range(TOPK):
                    settle(v.tensor_tensor(hot[:, k], iota8[:].unsqueeze(1).to_broadcast(full),
                                           topf[:, :, k:k + 1].to_broadcast(full), ALU.is_equal))
                v.tensor_tensor(both[:], hot[:, 0], hot[:, 1], ALU.add).then_inc(both_ready, 1)
                dve.wait_ge(ranks_ready, r + 1)
                settle(v.tensor_copy(tot[:], bank[:, 6, 128:128 + NT * NE].rearrange("p (t e) -> p e t", e=NE)))
                flat = [t[:].rearrange("p e t -> p (e t)") for t in (keep, tot, incl)]
                settle(v.tensor_tensor_scan(out=flat[2], data0=flat[0], data1=flat[1], initial=0.0,
                                            op0=ALU.mult, op1=ALU.add))
                settle(v.tensor_scalar(over[:], iota_lane[:, 0:NT].unsqueeze(1).to_broadcast([P, NE, NT]), float(P), None, ALU.mult))
                settle(v.tensor_tensor(over[:], incl[:, :, NT - 1:NT].to_broadcast([P, NE, NT]), over[:], ALU.is_gt))
                settle(v.tensor_reduce(e_tiles[:], over[:], mybir.AxisListType.X, ALU.add))
                settle(v.tensor_tensor_scan(out=e_end[:], data0=ones[:, 0:NE], data1=e_tiles[:], initial=0.0,
                                            op0=ALU.mult, op1=ALU.add))
                settle(v.tensor_tensor(e_base[:], e_end[:], e_tiles[:], ALU.subtract))
                settle(v.tensor_scalar(e_base[:], e_base[:], float(P), None, ALU.mult))
                settle(v.tensor_tensor(incl[:], incl[:], tot[:], ALU.subtract))
                settle(v.tensor_tensor(incl[:], incl[:], e_base[:].unsqueeze(2).to_broadcast([P, NE, NT]), ALU.add))
                place = both[:]
                settle(v.tensor_tensor(place, bank[:, 6, 0:NT * NE].rearrange("p (t e) -> p t e", e=NE),
                                       incl[:].rearrange("p e t -> p t e"), ALU.add))
                for k in range(TOPK):
                    settle(v.tensor_tensor(hot[:, k], hot[:, k], place, ALU.mult))
                settle(v.tensor_reduce(slot[:], hot[:].rearrange("p k t e -> p (k t) e"), mybir.AxisListType.X, ALU.add))
                settle(v.tensor_copy(slot_i[:, 0, :], slot[:]))
                v.tensor_scalar(slot_i[:, 1, :], slot_i[:, 0, :], P - 1, None, ALU.bitwise_and)
                settle(v.tensor_scalar(slot_i[:, 2, :], slot_i[:, 0, :], P.bit_length() - 1, None, ALU.logical_shift_right))
                settle(v.tensor_copy(slot_f[:], slot_i[:, 1:3, :]))
                v.tensor_tensor(low_hot, iota_lane[:].unsqueeze(1).to_broadcast([P, NA, P]),
                                slot_f[:, 0, :].unsqueeze(2).to_broadcast([P, NA, P]), ALU.is_equal)
                settle(v.tensor_tensor(high_hot[:, :, 0, :], iota_lane[:, 0:STEPS].unsqueeze(1).to_broadcast([P, NA, STEPS]),
                                       slot_f[:, 1, :].unsqueeze(2).to_broadcast([P, NA, STEPS]), ALU.is_equal))
                v.tensor_scalar(high_hot[:, :, 1, :], high_hot[:, :, 0, :], lane[:, 0:1], None, ALU.mult)
                v.tensor_tensor(high_hot[:, :, 2, :], high_hot[:, :, 0, :],
                                iota_lane[:, 0:NA].unsqueeze(2).to_broadcast([P, NA, STEPS]), ALU.mult).then_inc(hot_ready, 1)
                wide = [P, STEPS, NE]
                settle(v.tensor_tensor(past[:], e_end[:].unsqueeze(1).to_broadcast(wide),
                                       iota_lane[:, 0:STEPS].unsqueeze(2).to_broadcast(wide), ALU.is_le))
                settle(v.tensor_reduce(expert_f[:], past[:], mybir.AxisListType.X, ALU.add))
                settle(v.tensor_scalar(expert_f[:], expert_f[:], float(NE - 1), None, ALU.min))
                v.tensor_copy(expert[:], expert_f[:])
                dve.wait_ge(found_ready, r + 1)
                settle(v.tensor_copy(found[:].rearrange("p a n -> p (a n)"), bank[:, 7, 0:3 * STEPS]))
                settle(v.scalar_tensor_tensor(out=dest_f[:], in0=found[:, 2, :], scalar=float(P), in1=found[:, 1, :],
                                              op0=ALU.mult, op1=ALU.add))
                settle(v.tensor_copy(dest[:], dest_f[:]))
                settle(v.tensor_scalar(source[:], dest[:], NT * P - 1, None, ALU.bitwise_and))
                settle(v.tensor_scalar(found[:, 0, :], found[:, 0, :], -float(NOWHERE), float(NOWHERE), ALU.mult, ALU.add))
                settle(v.tensor_tensor(dest_f[:], dest_f[:], found[:, 0, :], ALU.add))
                v.tensor_copy(dest[:], dest_f[:]).then_inc(plan_ready, 1)

                def mul(n, p):
                    dve.wait_ge(silu_done, n + 1 + AHEAD)
                    dve.wait_ge(turn_done, n + 1)
                    v.tensor_tensor(act[:, p, :], bank[:, 2 + p, :], sg[:, p, :], ALU.mult).then_inc(mul_done, 1)

                def take(n, k):
                    dve.wait_ge(row_free, n + 1)
                    dve.wait_ge(down_done, n + 1 + AHEAD)
                    v.tensor_copy(y_row[:, k % RING, :], bank[:, 6, 0:D]).then_inc(y_taken, 1)

                def step(n, k, first=False):
                    mul(n, k % 2)
                    if not first:
                        take(n - 1, k - 1)

                step(base, 0, first=True)
                with dve.Fori(0, STEPS // RING - 1) as q:
                    for k in range(1, RING + 1):
                        step(q * RING + (base + k), k)
                for k in range(STEPS - RING + 1, STEPS):
                    step(base + k, k)
                take(base + STEPS - 1, STEPS - 1)

                for g in range(NG):
                    dve.wait_ge(y_back[g], 16 * TOPK * (r + 1))
                    for k, src in ((0, normed), (1, x0)):
                        for j in range(GT * g, GT * (g + 1)):
                            ins = v.scalar_tensor_tensor(out=hid[:, j, :], in0=src[:, j, :], scalar=w[:, k, j:j + 1],
                                                         in1=hid[:, j, :], op0=ALU.mult, op1=ALU.add)
                        settle(ins)
                    now = slice(GT * g, GT * (g + 1))
                    ins = v.scalar_tensor_tensor(out=x[:, now, :], in0=hid[:, now, :], scalar=0.5, in1=x[:, now, :],
                                                 op0=ALU.mult, op1=ALU.add)
                settle(ins)
                dve.sem_inc(x_ready, 1)

            dve.wait_ge(x_in, 16)
            dve.wait_ge(consts, CONSTS)
            dve.sem_inc(mul_done, AHEAD)
            dve.sem_inc(y_taken, 1)
            ffn(0)

            layer_norm(MAMBA_LN, x, normed)
            dve.wait_ge(mamba_in, MAMBA_LOADS)
            dve.wait_ge(uz_used, NG)
            for h in range(NH):
                for k in range(KC - 1):
                    ins = v.scalar_tensor_tensor(out=u[:, h, :, :], in0=u_raw[:, h, :, k:k + L], scalar=conv_w[:, h, k:k + 1],
                                                 in1=u[:, h, :, :], op0=ALU.mult, op1=ALU.add)
                    if k < KC - 2:
                        settle(ins)
                ins.then_inc(conv_done, 1)
            for g in range(NG):
                hi = bc_hi[:, bass.ts(g, GW)]
                src = bank[0:96, 2 + g % 2, :]
                dve.wait_ge(bcx_ready, g + 1)
                settle(v.tensor_copy(hi, src))
                settle(v.tensor_tensor(bc_r1, src, hi, ALU.subtract))
                settle(v.tensor_copy(bc_mid[:], bc_r1))
                settle(v.tensor_tensor(bc_r2, bc_r1, bc_mid[:], ALU.subtract))
                v.tensor_copy(hi[32:64, :], bc_mid[32:64, :])
                v.tensor_copy(hi[64:96, :], bc_r2[64:96, :]).then_inc(bc_split, 1)
            for g in range(NG):
                tmp = sp_tmp[g % 2][:]
                dve.wait_ge(sp_ready, g + 1)
                if g > 1:
                    dve.wait_ge(dt_ready, g - 1)
                settle(v.tensor_scalar(tmp, sp_exp[g], 1.0, 1.0, ALU.add, ALU.subtract))
                settle(v.tensor_tensor(tmp, sp_exp[g], tmp, ALU.subtract))
                settle(v.tensor_tensor(tmp, tmp, sp_ln[g], ALU.add))
                v.tensor_tensor(sp_relu[g], tmp, sp_relu[g], ALU.add).then_inc(dt_ready, 1)
            for i in range(2):
                ins = v.memset(decay[i].rearrange("p h (b l) -> p h b l", l=L)[:, :, :, 0:1], 0.0)
            ins.then_inc(zero_ready, 1)
            dve.sem_inc(scan_done, AHEAD)
            dve.sem_inc(drive_done, AHEAD)
            dve.sem_inc(read_done, AHEAD)
            dve.sem_inc(y_used, 1)
            dve.sem_inc(x_added, 1)
            wide = [P, NH, GW]
            with dve.Fori(0, NG) as c:
                def scan(n):
                    m = c * NS + n
                    dve.wait_ge(read_done, m + 1)
                    dve.wait_ge(decay_ready, m + 1 + AHEAD)
                    dve.wait_ge(drive_done, m + 1 + AHEAD)
                    v.tensor_tensor_scan(out=state[:, n % 2, :], data0=decay[n % 2].rearrange("p h t -> p (h t)"),
                                         data1=drive[:, n % 2, :], initial=0.0, op0=ALU.mult, op1=ALU.add)\
                        .then_inc(scan_done, 1)
                scan(0)
                for n in range(NS):
                    m = c * NS + n
                    if n + 1 < NS:
                        scan(n + 1)
                    dve.wait_ge(scan_done, m + 1 + AHEAD)
                    dve.wait_ge(c_spread, m + 1)
                    dve.wait_ge(y_added, m + 1)
                    v.tensor_tensor(read[:, n % 2, :].rearrange("p (h t) -> p h t", h=NH),
                                    state[:, n % 2, :].rearrange("p (h t) -> p h t", h=NH),
                                    bank[:, 7, :].unsqueeze(1).to_broadcast(wide), ALU.mult).then_inc(read_done, 1)
                dve.wait_ge(y_added, c * NS + (NS + AHEAD))
                for h in range(NH):
                    uc = u[:, h, bass.ts(c, GB), :].rearrange("p b l -> p (b l)")
                    ins = v.scalar_tensor_tensor(out=yg[:, h, :], in0=uc, scalar=cols[:, 1, h:h + 1],
                                                 in1=bank[:, 4 + h, :], op0=ALU.mult, op1=ALU.add)
                ins.then_inc(y_used, 1)
                dve.wait_ge(y_used, c + 2)
                v.tensor_tensor(yg, yg, zs[:, :, bass.ts(c, GW)], ALU.mult).then_inc(yg_ready, 1)
                dve.wait_ge(proj_ready, c + 1)
                xc = x[:, bass.ts(c, GT), :].rearrange("p t d -> p (t d)")
                v.tensor_tensor(xc, bank[:, 7, :], xc, ALU.add).then_inc(x_added, 1)
            dve.wait_ge(x_added, NG + 1)
            dve.sem_inc(x_ready, 1)
            ffn(1)


def kernel(**inputs):
    import numpy as np
    import concourse.bacc as bacc
    from concourse.bass_utils import run_bass_kernel_spmd

    def of(name):
        return np.asarray(inputs["L0_" + name])

    wx = of("attn_W_x").reshape(NH, P, DR + 2 * NS).transpose(1, 0, 2)
    arrays = {
        "x": of("attn_x").reshape(NT * P, D),
        "ln_cols": np.stack([of("ffn_ln1_g"), of("ffn_ln1_b"), of("ffn_ln2_g"), of("ffn_ln2_b")], axis=1),
        "attn_w": of("ffn_attn_w").T,
        "router_w": of("ffn_gate_w").T,
        "gate_w": of("ffn_gate_proj").transpose(2, 0, 1),
        "up_w": of("ffn_up_proj").transpose(2, 0, 1),
        "down_w": of("ffn_down_proj").reshape(NE, D, NI, P).transpose(3, 0, 2, 1),
        "w_in": of("attn_W_in"),
        "conv_w": of("attn_conv_w").reshape(NH, P, KC).transpose(1, 0, 2),
        "cols": np.stack([of("attn_conv_b"), of("attn_D"), of("attn_b_dt")]).reshape(3, NH, P).transpose(2, 0, 1),
        "w_dtlr": wx[:, :, 0:DR],
        "w_bc": np.concatenate([wx[:, :, DR:]] * 3, axis=2),
        "w_dt": of("attn_W_dt"),
        "w_out": of("attn_W_out").reshape(NH, P, D).transpose(1, 0, 2),
        "A_log": of("attn_A_log"),
    }
    arrays = {"in_" + k: np.ascontiguousarray(v) for k, v in arrays.items()}
    nc = bacc.Bacc("TRN2", target_bir_lowering=False, num_devices=1)
    aps = {k[3:]: nc.dram_tensor(k, v.shape, mybir.dt.from_np(v.dtype), kind="ExternalInput").ap()
           for k, v in arrays.items()}
    out = nc.dram_tensor("out", (NT * P, D), F32, kind="ExternalOutput").ap()
    macaron(nc, aps, out)
    r = run_bass_kernel_spmd(nc, [arrays], core_ids=[0])
    return r.results[0]["out"].reshape(NB, L, D)
```

```python
from contextlib import ExitStack

import concourse.bass as bass
from concourse import mybir

ALU = mybir.AluOpType
ACT = mybir.ActivationFunctionType
F32 = mybir.dt.float32
BF16 = mybir.dt.bfloat16
U32 = mybir.dt.uint32

P = 128
D = 128
NT = 16
GT = 4
NG = NT // GT
GW = GT * P
NE = 8
FI = 512
NI = FI // P
DI = 256
NH = DI // P
NB = 8
L = 256
GB = GW // L
NS = 16
DR = 64
KC = 4
EPS = 1e-5
TOPK = 2
NA = TOPK * NT
RING = 4
STEPS = -(-((TOPK * NT * P - NE) // P + NE) // RING) * RING
BODY = 12
assert (STEPS - RING) % BODY == 0
POOL_TURNS = 4
assert (STEPS // RING - 2) % POOL_TURNS == 0
NOWHERE = TOPK * NT * P
DRIVES = 4
STATES = 4
B_ROWS = 4
AHEAD = 2


def macaron(nc, a, out):
    ctx = ExitStack()
    with ctx:
        def sb(name, shape, dt=F32):
            return ctx.enter_context(nc.sbuf_tensor(name, shape, dt))

        def sem(name):
            return ctx.enter_context(nc.semaphore(name))

        bank = ctx.enter_context(nc.psum_tensor("bank", [P, 8, 512], F32))
        x = sb("x", [P, NT, D])
        normed = sb("normed", [P, NT, D])
        x0 = sb("x0", [P, NT, D])
        hid = sb("hid", [P, NT, D])
        aT = sb("aT", [P, NT * P])
        tT = sb("tT", [P, NT * P])
        gate_w = sb("gate_w", [P, NE, FI])
        up_w = sb("up_w", [P, NE, FI])
        down_w = sb("down_w", [P, NE, NI, D])
        attn_w = sb("attn_w", [P, D])
        router_w = sb("router_w", [P, NE])
        ln_cols = sb("ln_cols", [P, 4])
        ident = sb("ident", [P, P])
        iota8 = sb("iota8", [P, NE])
        eps = sb("eps", [P, 1])
        stats = sb("stats", [P, NT, 6])
        mv = sb("mv", [P, NT, 2])
        std = sb("std", [P, NT])
        rstd = sb("rstd", [P, NT])
        logits = sb("logits", [P, NT, NE])
        top = sb("top", [P, NT, 8])
        topi = sb("topi", [P, NT, 8], U32)
        topf = sb("topf", [P, NT, 2])
        gap = sb("gap", [P, NT])
        ew = sb("ew", [P, NT])
        w = sb("w", [P, 2, NT])
        rows = sb("rows", [P, RING, D])
        tile = sb("tile", [P, 2, P])
        y_row = sb("y_row", [P, RING, D])
        upper = sb("upper", [P, P])
        ones = sb("ones", [P, P])
        iota_lane = sb("iota_lane", [P, P])
        lane = sb("lane", [P, 1])
        hot = sb("hot", [P, TOPK, NT, NE])
        both = sb("both", [P, NT, NE])
        tot = sb("tot", [P, NE, NT])
        incl = sb("incl", [P, NE, NT])
        keep = sb("keep", [P, NE, NT])
        over = sb("over", [P, NE, NT])
        e_tiles = sb("e_tiles", [P, NE])
        e_end = sb("e_end", [P, NE])
        e_base = sb("e_base", [P, NE])
        slot = sb("slot", [P, NA])
        slot_i = sb("slot_i", [P, 3, NA], U32)
        slot_f = sb("slot_f", [P, 2, NA])
        found = sb("found", [P, 3, STEPS])
        dest_f = sb("dest_f", [P, STEPS])
        dest = sb("dest", [P, STEPS], U32)
        source = sb("source", [P, STEPS], U32)
        dest_now = sb("dest_now", [P, RING], U32)
        source_now = sb("source_now", [P, RING], U32)
        past = sb("past", [P, STEPS, NE])
        expert_f = sb("expert_f", [P, STEPS])
        expert = sb("expert", [P, STEPS], mybir.dt.int32)
        sg = sb("sg", [P, 2, FI])
        act = sb("act", [P, 2, FI])
        actT = sb("actT", [P, 2, FI])
        w_in = sb("w_in", [P, 2 * DI])
        conv_w = sb("conv_w", [P, NH, KC])
        cols = sb("cols", [P, 3, NH])
        w_dtlr = sb("w_dtlr", [P, NH, DR])
        w_bc = sb("w_bc", [P, NH, 3 * 2 * NS])
        w_dt = sb("w_dt", [DR, DI])
        w_out = sb("w_out", [P, NH, D])
        a_col = sb("a_col", [P, NS])
        u_raw = sb("u_raw", [P, NH, NB, L + KC - 1])
        dt = u_raw[:, :, :, KC - 1:]
        u = sb("u", [P, NH, NB, L])
        zs = sb("zs", [P, NH, NT * P])
        dtu = sb("dtu", [P, NH, NT * P])
        dtlr = tT[0:DR, :]
        hots = dtu[:].rearrange("p h n -> p (h n)").bitcast(BF16)
        low_hot = hots[:, 0:NA * P].rearrange("p (c n) -> p c n", c=NA)
        high_hot = hots[:, NA * P:NA * (P + 3 * STEPS)].rearrange("p (c a n) -> p c a n", c=NA, a=3)
        bc_hi = sb("bc_hi", [96, NT * P], BF16)
        bc_mid = sb("bc_mid", [96, GW], BF16)
        bc_r1, bc_r2 = actT[0:96, 0, :], actT[0:96, 1, :]
        sel = sb("sel", [96, 2 * NS, P], BF16)

        def scan_buffer(t):
            return t[:].rearrange("p a b -> p (a b)").rearrange("p (s n) -> p s n", s=2)
        b_row = normed[:].rearrange("p t d -> p (t d)").rearrange("p (s n) -> p s n", s=B_ROWS)
        drive_lo = scan_buffer(x0)
        drive = [drive_lo[:, 0, :], drive_lo[:, 1, :], sg[:].rearrange("p a n -> p (a n)"), act[:].rearrange("p a n -> p (a n)")]
        state_lo = scan_buffer(hid)
        state = [state_lo[:, 0, :], state_lo[:, 1, :], aT[:, NH * GW:], actT[:].rearrange("p a n -> p (a n)")]
        read = tT[:].rearrange("p (s n) -> p s n", s=2)
        sp_exp = [dtu[:, :, bass.ts(g, GW)] for g in range(NG)]
        sp_relu = [dt[:, :, GB * g:GB * (g + 1), :] for g in range(NG)]
        sp_ln = [(state_lo, drive_lo)[g // 2][:, g % 2, :].rearrange("p (h n) -> p h n", h=NH) for g in range(NG)]
        sp_tmp = [sg[:], act[:]] + [read[:, i, :].rearrange("p (h n) -> p h n", h=NH) for i in range(2)]
        yg = aT[:, 0:NH * GW].rearrange("p (s n) -> p s n", s=NH)
        decay = [bank[:, 2 * i:2 * i + 2, :] for i in range(2)]

        t_rows = nc.dram_tensor("t_rows", [NT * P, D], F32, kind="Internal").ap()
        y_rows = nc.dram_tensor("y_rows", [TOPK * NT * P, D], F32, kind="Internal").ap()

        t_out = sem("t_out")
        gathered = [sem(f"gathered{b}") for b in range(RING)]
        y_sent = [sem(f"y_sent{b}") for b in range(RING)]
        y_back = [sem(f"y_back{g}") for g in range(NG)]
        both_ready = sem("both_ready"); ranks_ready = sem("ranks_ready"); hot_ready = sem("hot_ready")
        found_ready = sem("found_ready"); plan_ready = sem("plan_ready")
        in_turned = sem("in_turned"); in_taken = sem("in_taken"); y_taken = sem("y_taken")
        x_in = [sem(f"x_in{g}") for g in range(NG)]; small_in = sem("small_in"); big_in = sem("big_in"); mamba_in = sem("mamba_in")
        out_sent = sem("out_sent")
        consts = sem("consts"); pool_step = sem("pool_step")
        dve_step = sem("dve_step"); act_step = sem("act_step")
        var_ready = sem("var_ready"); std_ready = sem("std_ready"); normed_ready = sem("normed_ready")
        turned = sem("turned"); turned_used = sem("turned_used")
        attn_ready = sem("attn_ready"); attn_used = sem("attn_used")
        logits_ready = sem("logits_ready"); gap_ready = sem("gap_ready"); ew_ready = sem("ew_ready")
        gu_ready = sem("gu_ready"); silu_done = sem("silu_done")
        mul_done = sem("mul_done"); turn_done = sem("turn_done"); evac_done = sem("evac_done")
        down_done = sem("down_done")
        x_ready = sem("x_ready"); x_halved = sem("x_halved")
        u_raw_ready = sem("u_raw_ready"); u_raw_taken = sem("u_raw_taken"); z_ready = sem("z_ready"); z_taken = sem("z_taken")
        conv_done = sem("conv_done"); u_ready = sem("u_ready")
        bcx_ready = sem("bcx_ready"); bc_split = sem("bc_split"); dtlr_ready = sem("dtlr_ready")
        dtx_ready = sem("dtx_ready"); dtx_taken = sem("dtx_taken"); exp_ready = sem("exp_ready"); sp_ready = sem("sp_ready"); x_added = sem("x_added")
        dt_ready = sem("dt_ready"); wait_carrier = sem("wait_carrier"); row_free = sem("row_free"); zero_ready = sem("zero_ready"); index_ready = sem("index_ready"); decay_begun = sem("decay_begun")
        b_spread = sem("b_spread"); c_spread = sem("c_spread"); b_copied = sem("b_copied"); dtu_ready = sem("dtu_ready"); decay_ready = sem("decay_ready"); drive_done = sem("drive_done")
        scan_done = sem("scan_done"); read_done = sem("read_done"); y_added = sem("y_added")
        yg_ready = sem("yg_ready"); y_used = sem("y_used"); proj_ready = sem("proj_ready")

        block = ctx.enter_context(nc.Block())

        FFN_LN = [[0, 1, 2], [4, 5, 6]]
        MAMBA_LN = 3
        STAT_ORDER = []
        for k0, k1, k2 in FFN_LN:
            STAT_ORDER += [(k0, 0), (k0, 1), (k0, 2), (k1, 0), (k0, 3), (k1, 1), (k1, 2), (k1, 3)]
            STAT_ORDER += [(k2, g) for g in range(NG)]
            if k0 < MAMBA_LN:
                STAT_ORDER += [(MAMBA_LN, g) for g in range(NG)]
        TURN = {1: 0, 2: 1, 3: 2, 5: 3, 6: 4}

        @block.sync
        def _(sp):
            x_view = a["x"].rearrange("(t p) d -> p t d", p=P)
            for g in range(NG):
                sp.dma_start(x[:, GT * g:GT * (g + 1), :], x_view[:, GT * g:GT * (g + 1), :]).then_inc(x_in[g], 16)
            sp.dma_start(ln_cols[:], a["ln_cols"]).then_inc(small_in, 16)
            sp.dma_start(attn_w[:], a["attn_w"]).then_inc(small_in, 16)
            sp.dma_start(router_w[:], a["router_w"]).then_inc(small_in, 16)
            sp.dma_start(gate_w[:], a["gate_w"]).then_inc(big_in, 16)
            sp.dma_start(up_w[:], a["up_w"]).then_inc(big_in, 16)
            sp.dma_start(down_w[:], a["down_w"]).then_inc(big_in, 16)
            sp.dma_start(w_in[:], a["w_in"]).then_inc(mamba_in, 16)
            sp.dma_start(conv_w[:], a["conv_w"]).then_inc(mamba_in, 16)
            sp.dma_start(cols[:], a["cols"]).then_inc(mamba_in, 16)
            sp.dma_start(w_dtlr[:], a["w_dtlr"]).then_inc(mamba_in, 16)
            sp.dma_start(w_bc[:], a["w_bc"]).then_inc(mamba_in, 16)
            sp.dma_start(w_dt[:], a["w_dt"]).then_inc(mamba_in, 16)
            sp.dma_start(w_out[:], a["w_out"]).then_inc(mamba_in, 16)
            sp.dma_start(a_col[:], a["A_log"].partition_broadcast(P)).then_inc(mamba_in, 16)
            for r in range(2):
                sp.wait_ge(normed_ready, NG * (TURN[FFN_LN[r][2]] + 1))
                sp.dma_start(t_rows.rearrange("(t p) d -> p t d", p=P), normed[:]).then_inc(t_out, 16)
                for b in range(RING):
                    sp.wait_ge(y_sent[b], 16 * (r + 1) * STEPS // RING)
                y_view = y_rows.rearrange("(k g t p) d -> g k p t d", k=TOPK, g=NG, p=P)
                for g in range(NG):
                    for k, dst in ((0, normed), (1, x0)):
                        sp.dma_start(dst[:, GT * g:GT * (g + 1), :], y_view[g, k]).then_inc(y_back[g], 16)
            out_view = out.rearrange("(t p) d -> p t d", p=P)
            for g in range(NG):
                sp.wait_ge(x_ready, NG + g + 1)
                sp.dma_start(out_view[:, GT * g:GT * (g + 1), :], x[:, GT * g:GT * (g + 1), :]).then_inc(out_sent, 16)
            sp.wait_ge(out_sent, 16 * NG)
        MAMBA_LOADS = 16 * 8
        CONSTS = 9
        SEL = 7

        @block.gpsimd
        def _(pool):
            g = nc.gpsimd
            g.memset(eps[:], EPS).then_inc(consts, 1)
            g.memset(ident[:], 0.0).then_inc(pool_step, 1)
            g.iota(iota8[:], [[1, NE]], base=0, channel_multiplier=0, allow_small_or_imprecise_dtypes=True).then_inc(consts, 1)
            g.memset(u_raw[:, :, :, 0:KC - 1], 0.0).then_inc(consts, 1)
            g.memset(ones[:], 1.0).then_inc(consts, 1)
            g.memset(upper[:], 1.0).then_inc(pool_step, 1)
            g.memset(keep[:], 1.0).then_inc(pool_step, 1)
            g.iota(iota_lane[:], [[1, P]], base=0, channel_multiplier=0, allow_small_or_imprecise_dtypes=True).then_inc(consts, 1)
            g.iota(lane[:], [[0, 1]], base=0, channel_multiplier=1, allow_small_or_imprecise_dtypes=True).then_inc(consts, 1)
            pool.wait_ge(pool_step, 3)
            g.memset(keep[:, :, 0:1], 0.0).then_inc(consts, 1)
            g.affine_select(out=upper[:], in_=upper[:], compare_op=ALU.is_gt, fill=0.0, base=0,
                            pattern=[[1, P]], channel_multiplier=-1).then_inc(consts, 1)
            g.affine_select(out=ident[:], in_=ident[:], compare_op=ALU.not_equal, fill=1.0, base=0,
                            pattern=[[-1, P]], channel_multiplier=1).then_inc(consts, 1)
            g.memset(sel[:], 0.0).then_inc(pool_step, 1)
            for part in range(3):
                pool.wait_ge(pool_step, 4 + part)
                g.affine_select(out=sel[:], in_=sel[:], compare_op=ALU.not_equal, fill=1.0, base=-32 * part,
                                pattern=[[-1, 2 * NS], [0, P]], channel_multiplier=1).then_inc(pool_step, 1)

            def gather_and_scatter(r):
                base = STEPS * r

                def gather(b):
                    g.indirect_dma_start(out=rows[:, b, :], out_offset=None, in_=t_rows,
                                         in_offset=bass.IndirectOffsetOnAxis(ap=source_now[:, b:b + 1], axis=0),
                                         bounds_check=NT * P - 1, oob_is_err=False).then_inc(gathered[b], 16)

                def scatter(n, b):
                    pool.wait_ge(y_taken, n + (base + 2))
                    pool.sem_inc(wait_carrier, 1)
                    g.indirect_dma_start(out=y_rows, out_offset=bass.IndirectOffsetOnAxis(ap=dest_now[:, b:b + 1], axis=0),
                                         in_=y_row[:, b, :], in_offset=None,
                                         bounds_check=NOWHERE - 1, oob_is_err=False).then_inc(y_sent[b], 16)

                def index(of, now, n, b):
                    g.tensor_copy(now[:, b:b + 1], of[:, bass.ds(n, 1)]).then_inc(index_ready, 1)

                pool.wait_ge(plan_ready, r + 1)
                pool.wait_ge(t_out, 16 * (r + 1))
                t0 = 16 * (base // RING)
                for b in range(RING):
                    index(source, source_now, b, b)
                    pool.wait_ge(index_ready, 2 * base + b + 1)
                    gather(b)
                def turn(q, gather_more=True):
                    for b in range(RING):
                        n = q * RING + b
                        if gather_more:
                            pool.wait_ge(gathered[b], q * 16 + (t0 + 16))
                            index(source, source_now, n + RING, b)
                        if not (r == 0 and isinstance(q, int) and q == 0):
                            pool.wait_ge(y_sent[b], q * 16 + t0)
                        pool.sem_inc(row_free, 1)
                        index(dest, dest_now, n, b)
                        if gather_more:
                            pool.wait_ge(index_ready, n * 2 + (2 * base + RING + 2))
                            pool.wait_ge(in_turned, n + (base + 1))
                            pool.sem_inc(wait_carrier, 1)
                            gather(b)
                        else:
                            pool.wait_ge(index_ready, n + (2 * base + STEPS + 1))
                        scatter(n, b)

                turn(0)
                with pool.Fori(0, (STEPS // RING - 2) // POOL_TURNS) as q:
                    for i in range(POOL_TURNS):
                        turn(q * POOL_TURNS + (i + 1))
                turn(STEPS // RING - 1, gather_more=False)

            gather_and_scatter(0)
            for gq in range(NG):
                pool.wait_ge(dt_ready, gq + 1)
                g.tensor_tensor(dtu[:, :, bass.ts(gq, GW)].rearrange("p h (b l) -> p h b l", l=L),
                                dt[:, :, GB * gq:GB * (gq + 1), :], u[:, :, GB * gq:GB * (gq + 1), :], ALU.mult)\
                    .then_inc(dtu_ready, 1)
            pool.wait_ge(dtu_ready, NG)
            with pool.Fori(0, NG) as c:
                for n in range(NS):
                    m = c * NS + n
                    pool.wait_ge(b_copied, m + 1 + 1)
                    pool.wait_ge(scan_done, m + 1)
                    pool.sem_inc(wait_carrier, 1)
                    g.tensor_tensor(drive[n % DRIVES].rearrange("p (h t) -> p h t", h=NH), dtu[:, :, bass.ts(c, GW)],
                                    b_row[:, n % B_ROWS, :].unsqueeze(1).to_broadcast([P, NH, GW]), ALU.mult).then_inc(drive_done, 1)
            gather_and_scatter(1)

        @block.scalar
        def _(eng):
            s = nc.scalar

            def std_of(k, g):
                now = slice(GT * g, GT * (g + 1))
                eng.wait_ge(var_ready, STAT_ORDER.index((k, g)) + 1)
                s.activation(std[:, now], mv[:, now, 1], ACT.Sqrt, bias=eps[:, 0:1]).then_inc(std_ready, 1)

            def turned_out(k, g, dst, scale, bias):
                n = NG * TURN[k] + g
                eng.wait_ge(turned, n + 1)
                s.activation(dst[:, bass.ts(g, GW)], bank[:, n % 2, :], ACT.Identity, bias=bias, scale=scale)\
                    .then_inc(turned_used, 1)

            def ffn(r):
                base = STEPS * r
                k0, k1, k2 = FFN_LN[r]

                def turned_1(g):
                    turned_out(k1, g, aT, ln_cols[:, 0:1], ln_cols[:, 1:2])

                def turned_2(g):
                    turned_out(k2, g, tT, ln_cols[:, 2:3], ln_cols[:, 3:4])

                for k, g in ((k0, 0), (k0, 1), (k0, 2), (k1, 0), (k0, 3), (k1, 1), (k1, 2)):
                    std_of(k, g)
                if r == 0:
                    eng.wait_ge(small_in, 16 * 3)
                turned_1(0)
                std_of(k1, 3)
                turned_1(1)
                std_of(k2, 0)
                turned_1(2)
                std_of(k2, 1)
                turned_1(3)
                std_of(k2, 2)
                turned_2(0)
                std_of(k2, 3)
                for g in range(1, NG):
                    turned_2(g)
                eng.wait_ge(gap_ready, r + 1)
                s.activation(ew[:], gap[:], ACT.Exp).then_inc(ew_ready, 1)

                def silu(n, p):
                    eng.wait_ge(gu_ready, n + 1)
                    eng.wait_ge(mul_done, n + 1)
                    s.activation(sg[:, p, :], bank[:, p, :], ACT.Silu).then_inc(silu_done, 1)

                def evac(n, p):
                    eng.wait_ge(turn_done, n + 1 + AHEAD)
                    eng.wait_ge(down_done, n + 1)
                    s.activation(actT[:, p, :], bank[:, 4 + p, :], ACT.Copy).then_inc(evac_done, 1)

                def take_in(n, p):
                    eng.wait_ge(in_turned, n + 1)
                    s.activation(tile[:, p, :], bank[:, 7, 0:P], ACT.Identity, bias=ln_cols[:, 3:4], scale=ln_cols[:, 2:3])\
                        .then_inc(in_taken, 1)

                def step(n, k, ahead=2):
                    if ahead > 0:
                        silu(n + 1, (k + 1) % 2)
                    if ahead > 1:
                        take_in(n + 2, k % 2)
                    evac(n, k % 2)

                take_in(base, 0)
                take_in(base + 1, 1)
                silu(base, 0)
                step(base, 0)
                with eng.Fori(0, (STEPS - RING) // BODY) as q:
                    for k in range(1, BODY + 1):
                        step(q * BODY + (base + k), k)
                for k in range(1, RING):
                    step(base + STEPS - RING + k, k, RING - 1 - k)

            eng.wait_ge(consts, 1)
            eng.sem_inc(silu_done, AHEAD)
            eng.sem_inc(evac_done, AHEAD)
            eng.sem_inc(in_taken, 1)
            ffn(0)

            std_of(MAMBA_LN, 0)
            for g in range(NG):
                if g + 1 < NG:
                    std_of(MAMBA_LN, g + 1)
                turned_out(MAMBA_LN, g, aT, 1.0, 0.0)
            eng.wait_ge(mamba_in, MAMBA_LOADS)
            def halves_out(g):
                eng.wait_ge(u_raw_ready, g + 1)
                for h in range(NH):
                    s.activation(u_raw[:, h, GB * g:GB * (g + 1), KC - 1:],
                                 bank[:, 4 + h, :].rearrange("p (b l) -> p b l", l=L), ACT.Copy)
                    ins = s.activation(u[:, h, GB * g:GB * (g + 1), :].rearrange("p b l -> p (b l)"), bank[:, 4 + h, :],
                                       ACT.Identity, bias=cols[:, 0, h:h + 1], scale=conv_w[:, h, KC - 1:KC])
                ins.then_inc(u_raw_taken, 1)
                eng.wait_ge(z_ready, g + 1)
                for h in range(NH):
                    ins = s.activation(zs[:, h, bass.ts(g, GW)], bank[:, 6 + h, :], ACT.Silu)
                ins.then_inc(z_taken, 1)

            def silu_u(g):
                eng.wait_ge(conv_done, g + 1)
                ug = u[:, :, GB * g:GB * (g + 1), :]
                s.activation(ug, ug, ACT.Silu).then_inc(u_ready, 1)

            def dtlr_out(g):
                eng.wait_ge(bcx_ready, g + 1)
                s.activation(dtlr[:, bass.ts(g, GW)], bank[0:DR, 0, :], ACT.Copy).then_inc(dtlr_ready, 1)

            def dt_out(g):
                eng.wait_ge(dtx_ready, g + 1)
                eng.wait_ge(conv_done, g + 1)
                for h in range(NH):
                    s.activation(sp_exp[g][:, h, :], bank[:, 2 + h, :], ACT.Abs, bias=cols[:, 2, h:h + 1])
                for h in range(NH):
                    ins = s.activation(sp_relu[g][:, h], bank[:, 2 + h, :].rearrange("p (b l) -> p b l", l=L), ACT.Relu, bias=cols[:, 2, h:h + 1])
                ins.then_inc(dtx_taken, 1)

            halves_out(0)
            halves_out(1)
            silu_u(0)
            halves_out(2)
            silu_u(1)
            dtlr_out(0)
            halves_out(3)
            silu_u(2)
            dt_out(0)
            dtlr_out(1)
            silu_u(3)
            dt_out(1)
            for g in range(2, NG):
                dtlr_out(g)
                dt_out(g)
            s.activation(a_col[:], a_col[:], ACT.Exp).then_inc(act_step, 1)
            eng.wait_ge(act_step, 1)
            s.activation(a_col[:], a_col[:], ACT.Copy, scale=-1.0).then_inc(act_step, 1)
            for g in range(NG):
                eng.wait_ge(dtx_taken, g + 1)
                s.activation(sp_exp[g], sp_exp[g], ACT.Exp, scale=-1.0).then_inc(exp_ready, 1)
            for g in range(NG):
                eng.wait_ge(exp_ready, g + 1)
                s.activation(sp_ln[g], sp_exp[g], ACT.Ln, bias=1.0).then_inc(sp_ready, 1)
            eng.wait_ge(zero_ready, 1)
            eng.sem_inc(decay_ready, AHEAD)
            eng.sem_inc(b_copied, 1)
            s.preload_act_table(ACT.Exp)
            with eng.Fori(0, NG) as c:
                for n in range(NS):
                    m = c * NS + n
                    eng.wait_ge(b_spread, m + 1)
                    eng.wait_ge(drive_done, m + 1)
                    s.activation(b_row[:, n % B_ROWS, :], bank[:, 6, :], ACT.Copy).then_inc(b_copied, 1)
                    eng.wait_ge(scan_done, m + (1 + DRIVES - AHEAD))
                    eng.sem_inc(decay_begun, 1)
                    out_v = decay[n % 2].rearrange("p h (b l) -> p h b l", l=L)
                    s.activation(out_v[:, :, :, 1:L], dt[:, :, bass.ts(c, GB), 1:L],
                                 ACT.Exp, scale=a_col[:, n:n + 1]).then_inc(decay_ready, 1)
            ffn(1)

        @block.tensor
        def _(pe):
            t = nc.tensor

            def turn_group(k, g):
                n = NG * TURN[k] + g
                pe.wait_ge(normed_ready, n + 1)
                if n >= 2:
                    pe.wait_ge(turned_used, n - 1)
                for i in range(GT):
                    ins = t.transpose(bank[:, n % 2, bass.ts(i, P)], normed[:, GT * g + i, :], ident[:])
                ins.then_inc(turned, 1)

            def ffn(r):
                base = STEPS * r
                k1, k2 = FFN_LN[r][1:]
                turn_group(k1, 0)
                for g in range(NG):
                    if g + 1 < NG:
                        turn_group(k1, g + 1)
                    n = NG * r + g
                    pe.wait_ge(turned_used, NG * TURN[k1] + g + 1)
                    if n >= 2:
                        pe.wait_ge(attn_used, n - 1)
                    for i in range(GT):
                        ins = t.matmul(bank[:, 2 + g % 2, bass.ts(i, P)], aT[:, bass.ts(GT * g + i, P)], attn_w[:],
                                       start=True, stop=True)
                    ins.then_inc(attn_ready, 1)
                turn_group(k2, 0)
                for g in range(NG):
                    if g + 1 < NG:
                        turn_group(k2, g + 1)
                    pe.wait_ge(turned_used, NG * TURN[k2] + g + 1)
                    for i in range(GT):
                        j = GT * g + i
                        ins = t.matmul(bank[:, 7, bass.ts(j, NE)], tT[:, bass.ts(j, P)], router_w[:],
                                       start=True, stop=True)
                ins.then_inc(logits_ready, 1)
                pe.wait_ge(both_ready, r + 1)
                pe_flat = both[:].rearrange("p t e -> p (t e)")
                t.matmul(bank[:, 6, 0:NT * NE], upper[:], pe_flat, start=True, stop=True)
                t.matmul(bank[:, 6, 128:128 + NT * NE], ones[:], pe_flat, start=True, stop=True).then_inc(ranks_ready, 1)
                for c in range(NA):
                    if c % (NA // NG) == 0:
                        pe.wait_ge(hot_ready, NG * r + c // (NA // NG) + 1)
                    ins = t.matmul(bank[:, 7, 0:3 * STEPS], low_hot[:, c, :],
                                   high_hot[:, c, :, :].rearrange("p a n -> p (a n)"), start=(c == 0), stop=(c == NA - 1))
                ins.then_inc(found_ready, 1)

                def turn_in(n, k, turn):
                    pe.wait_ge(gathered[k % RING], turn)
                    pe.wait_ge(in_taken, n + 1)
                    t.transpose(bank[:, 7, 0:P], rows[:, k % RING, :], ident[:]).then_inc(in_turned, 1)

                def expert_of(m):
                    return pe.value_load(expert[0:1, bass.ds(m, 1)], min_val=0, max_val=NE - 1)

                def gate_up(n, k, e):
                    pe.wait_ge(in_taken, n + 1 + 1)
                    pe.wait_ge(silu_done, n + 1)
                    pe.wait_ge(mul_done, n + 1)
                    t.matmul(bank[:, k % 2, :], tile[:, k % 2, :], gate_w[:, bass.ds(e, 1), :].rearrange("p a n -> p (a n)"),
                             start=True, stop=True)
                    t.matmul(bank[:, 2 + k % 2, :], tile[:, k % 2, :], up_w[:, bass.ds(e, 1), :].rearrange("p a n -> p (a n)"),
                             start=True, stop=True).then_inc(gu_ready, 1)

                def turn(n, p):
                    pe.wait_ge(mul_done, n + 1 + AHEAD)
                    pe.wait_ge(evac_done, n + 1)
                    for i in range(NI):
                        ins = t.transpose(bank[:, 4 + p, bass.ts(i, P)], act[:, p, bass.ts(i, P)], ident[:])
                    ins.then_inc(turn_done, 1)

                def down(n, p, e):
                    pe.wait_ge(evac_done, n + 1 + AHEAD)
                    pe.wait_ge(y_taken, n + 1)
                    for i in range(NI):
                        ins = t.matmul(bank[:, 6, 0:D], actT[:, p, bass.ts(i, P)],
                                       down_w[:, bass.ds(e, 1), i, :].rearrange("p a n -> p (a n)"),
                                       start=(i == 0), stop=(i == NI - 1))
                    ins.then_inc(down_done, 1)

                def steps_of(m0, k0, count, turns, last=False):
                    known = {k0 + i: expert_of(m0 + i) for i in (-1, 0, 1) if m0 is not None and (i >= 0 or k0 > 0) and
                             not (last and count == 0)}
                    for i in range(count):
                        m, k = m0 + i, k0 + i
                        n = m + base
                        ahead = 2 if not last else count - 1 - i
                        if ahead > 0:
                            gate_up(n + 1, k + 1, known[k + 1])
                        if i + 1 < count and ahead > 1:
                            known[k + 2] = expert_of(m + 2)
                        turn(n, k % 2)
                        if ahead > 1:
                            turn_in(n + 2, k + 2, turns((k + 2) // RING))
                        if k > 0:
                            down(n - 1, (k - 1) % 2, known[k - 1])
                    return known

                pe.wait_ge(plan_ready, r + 1)
                pe.wait_ge(big_in, 16 * 3)
                t0 = 16 * (base // RING)
                turn_in(base, 0, t0 + 16)
                turn_in(base + 1, 1, t0 + 16)
                gate_up(base, 0, expert_of(0))
                steps_of(0, 0, 1, lambda d: t0 + 16 * d + 16)
                with pe.Fori(0, (STEPS - RING) // BODY) as q:
                    steps_of(q * BODY + 1, 1, BODY, lambda d: q * (16 * BODY // RING) + (t0 + 16 * d + 16))
                known = steps_of(STEPS - RING + 1, STEPS - RING + 1, RING - 1, lambda d: t0 + 16 * d + 16, last=True)
                down(base + STEPS - 1, (STEPS - 1) % 2, known[STEPS - 1])

            pe.wait_ge(consts, CONSTS)
            pe.wait_ge(small_in, 16 * 3)
            pe.sem_inc(turn_done, AHEAD)
            pe.sem_inc(down_done, AHEAD)
            ffn(0)

            def in_project(g):
                pe.wait_ge(turned_used, NG * TURN[MAMBA_LN] + g + 1)
                if g > 0:
                    pe.wait_ge(u_raw_taken, g)
                for h in range(NH):
                    ins = t.matmul(bank[:, 4 + h, :], w_in[:, bass.ts(h, P)], aT[:, bass.ts(g, GW)], start=True, stop=True)
                ins.then_inc(u_raw_ready, 1)
                if g > 0:
                    pe.wait_ge(z_taken, g)
                for h in range(NH):
                    ins = t.matmul(bank[:, 6 + h, :], w_in[:, bass.ts(NH + h, P)], aT[:, bass.ts(g, GW)], start=True, stop=True)
                ins.then_inc(z_ready, 1)

            def x_project(g):
                pe.wait_ge(u_ready, g + 1)
                if g == 0:
                    pe.wait_ge(turned_used, NG * (TURN[MAMBA_LN] + 1))
                else:
                    pe.wait_ge(dtlr_ready, g)
                    pe.wait_ge(bc_split, g)
                ug = [u[:, h, GB * g:GB * (g + 1), :].rearrange("p b l -> p (b l)") for h in range(NH)]
                for h in range(NH):
                    t.matmul(bank[0:DR, 0, :], w_dtlr[:, h, :], ug[h], start=(h == 0), stop=(h == NH - 1))
                for h in range(NH):
                    ins = t.matmul(bank[0:96, 1, :], w_bc[:, h, :], ug[h], start=(h == 0), stop=(h == NH - 1))
                ins.then_inc(bcx_ready, 1)

            def dt_project(g):
                pe.wait_ge(dtlr_ready, g + 1)
                if g > 0:
                    pe.wait_ge(dtx_taken, g)
                for h in range(NH):
                    ins = t.matmul(bank[:, 2 + h, :], w_dt[:, bass.ts(h, P)], dtlr[:, bass.ts(g, GW)], start=True, stop=True)
                ins.then_inc(dtx_ready, 1)

            turn_group(MAMBA_LN, 0)
            turn_group(MAMBA_LN, 1)
            pe.wait_ge(mamba_in, MAMBA_LOADS)
            in_project(0)
            turn_group(MAMBA_LN, 2)
            turn_group(MAMBA_LN, 3)
            in_project(1)
            in_project(2)
            x_project(0)
            in_project(3)
            dt_project(0)
            for g in range(1, NG):
                x_project(g)
                dt_project(g)
            pe.wait_ge(bc_split, NG)
            pe.wait_ge(z_taken, NG)
            pe.wait_ge(pool_step, SEL)
            pe.sem_inc(y_added, AHEAD)
            def bc_of(c, n):
                return bc_hi[:, bass.ds(c * GW + n // NS * GW, GW)]

            def spread_b(c, n):
                pe.wait_ge(b_copied, c * NS + (n + 1))
                t.matmul(bank[:, 6, :], sel[:, n % NS, :], bc_of(c, n), start=True, stop=True).then_inc(b_spread, 1)

            def spread_c(c, n):
                pe.wait_ge(read_done, c * NS + (n + STATES))
                t.matmul(bank[:, 7, :], sel[:, NS + n % NS, :], bc_of(c, n), start=True, stop=True).then_inc(c_spread, 1)

            def add(c, n):
                pe.wait_ge(read_done, c * NS + (n + 1 + STATES))
                if n == 0:
                    pe.wait_ge(x_added, c + 1)
                for h in range(NH):
                    ins = t.matmul(bank[:, 4 + h, :], ident[:], read[:, n % 2, bass.ts(h, GW)],
                                   start=(n == 0), stop=(n == NS - 1))
                ins.then_inc(y_added, 1)

            def chunk(c, last):
                for n in range(1, NS):
                    if not (last and n + B_ROWS >= NS):
                        spread_b(c, n + B_ROWS)
                    spread_c(c, n)
                    add(c, n - 1)
                add(c, NS - 1)
                if not last:
                    spread_c(c, NS)
                    spread_b(c, NS + B_ROWS)
                pe.wait_ge(yg_ready, c + 1)
                for i in range(GT):
                    for h in range(NH):
                        ins = t.matmul(bank[:, 4, bass.ts(i, P)], yg[:, h, bass.ts(i, P)], w_out[:, h, :],
                                       start=(h == 0), stop=(h == NH - 1))
                ins.then_inc(proj_ready, 1)

            for n in range(B_ROWS):
                spread_b(0, n)
            spread_c(0, 0)
            spread_b(0, B_ROWS)
            with pe.Fori(0, NG - 1) as c:
                chunk(c, last=False)
            chunk(NG - 1, last=True)
            ffn(1)

        @block.vector
        def _(dve):
            v = nc.vector
            count = [0]

            def settle(ins):
                count[0] += 1
                ins.then_inc(dve_step, 1)
                dve.wait_ge(dve_step, count[0])

            def measure(k, g, src):
                for j in range(GT * g, GT * (g + 1)):
                    ins = v.bn_stats(stats[:, j, :], src[:, j, :])
                settle(ins)
                for j in range(GT * g, GT * (g + 1)):
                    ins = v.bn_aggr(mv[:, j, :], stats[:, j, :])
                ins.then_inc(var_ready, 1)

            def normalise(k, g, src, dst):
                now = slice(GT * g, GT * (g + 1))
                dve.wait_ge(std_ready, STAT_ORDER.index((k, g)) + 1)
                settle(v.reciprocal(rstd[:, now], std[:, now]))
                for j in range(GT * g, GT * (g + 1)):
                    ins = v.tensor_scalar(dst[:, j, :], src[:, j, :], mv[:, j, 0:1], rstd[:, j:j + 1],
                                          ALU.subtract, ALU.mult)
                if k in TURN:
                    ins.then_inc(normed_ready, 1)
                else:
                    settle(ins)

            def ffn(r):
                base = STEPS * r
                k0, k1, k2 = FFN_LN[r]
                def measure_0(g):
                    if r == 0:
                        dve.wait_ge(x_in[g], 16)
                    measure(k0, g, x)

                def add_attn(g):
                    dve.wait_ge(attn_ready, NG * r + g + 1)
                    settle(v.tensor_tensor(hid[:, GT * g:GT * (g + 1), :],
                                           bank[:, 2 + g % 2, :].rearrange("p (t d) -> p t d", d=D),
                                           x0[:, GT * g:GT * (g + 1), :], ALU.add))
                    dve.sem_inc(attn_used, 1)

                measure_0(0)
                measure_0(1)
                normalise(k0, 0, x, x0)
                measure_0(2)
                normalise(k0, 1, x, x0)
                measure(k1, 0, x0)
                measure_0(3)
                normalise(k0, 2, x, x0)
                measure(k1, 1, x0)
                normalise(k1, 0, x0, normed)
                normalise(k0, 3, x, x0)
                measure(k1, 2, x0)
                normalise(k1, 1, x0, normed)
                measure(k1, 3, x0)
                normalise(k1, 2, x0, normed)
                normalise(k1, 3, x0, normed)
                for g in range(NG):
                    add_attn(g)
                    measure(k2, g, hid)
                    if g > 0:
                        normalise(k2, g - 1, hid, normed)
                normalise(k2, NG - 1, hid, normed)
                if r == 0:
                    dve.wait_ge(consts, CONSTS)
                dve.wait_ge(logits_ready, r + 1)
                settle(v.tensor_copy(logits[:].rearrange("p t e -> p (t e)"), bank[:, 7, 0:NT * NE]))
                for j in range(NT):
                    ins = v.max(top[:, j, :], logits[:, j, :])
                settle(ins)
                v.tensor_tensor(gap[:], top[:, :, 1], top[:, :, 0], ALU.subtract).then_inc(gap_ready, 1)
                for j in range(NT):
                    ins = v.max_index(topi[:, j, :], top[:, j, :], logits[:, j, :])
                settle(ins)
                settle(v.tensor_copy(topf[:], topi[:, :, 0:2]))
                dve.wait_ge(ew_ready, r + 1)
                settle(v.tensor_scalar(w[:, 1, :], ew[:], 1.0, None, ALU.add))
                settle(v.reciprocal(w[:, 0, :], w[:, 1, :]))
                settle(v.tensor_tensor(w[:, 1, :], w[:, 0, :], ew[:], ALU.mult))
                settle(v.tensor_scalar(w[:], w[:], 0.5, None, ALU.mult))
                full = [P, NT, NE]
                for k in range(TOPK):
                    settle(v.tensor_tensor(hot[:, k], iota8[:].unsqueeze(1).to_broadcast(full),
                                           topf[:, :, k:k + 1].to_broadcast(full), ALU.is_equal))
                v.tensor_tensor(both[:], hot[:, 0], hot[:, 1], ALU.add).then_inc(both_ready, 1)
                dve.wait_ge(ranks_ready, r + 1)
                settle(v.tensor_copy(tot[:], bank[:, 6, 128:128 + NT * NE].rearrange("p (t e) -> p e t", e=NE)))
                flat = [t[:].rearrange("p e t -> p (e t)") for t in (keep, tot, incl)]
                settle(v.tensor_tensor_scan(out=flat[2], data0=flat[0], data1=flat[1], initial=0.0,
                                            op0=ALU.mult, op1=ALU.add))
                settle(v.tensor_scalar(over[:], iota_lane[:, 0:NT].unsqueeze(1).to_broadcast([P, NE, NT]), float(P), None, ALU.mult))
                settle(v.tensor_tensor(over[:], incl[:, :, NT - 1:NT].to_broadcast([P, NE, NT]), over[:], ALU.is_gt))
                settle(v.tensor_reduce(e_tiles[:], over[:], mybir.AxisListType.X, ALU.add))
                settle(v.tensor_tensor_scan(out=e_end[:], data0=ones[:, 0:NE], data1=e_tiles[:], initial=0.0,
                                            op0=ALU.mult, op1=ALU.add))
                settle(v.tensor_tensor(e_base[:], e_end[:], e_tiles[:], ALU.subtract))
                settle(v.tensor_scalar(e_base[:], e_base[:], float(P), None, ALU.mult))
                settle(v.tensor_tensor(incl[:], incl[:], tot[:], ALU.subtract))
                settle(v.tensor_tensor(incl[:], incl[:], e_base[:].unsqueeze(2).to_broadcast([P, NE, NT]), ALU.add))
                place = both[:]
                settle(v.tensor_tensor(place, bank[:, 6, 0:NT * NE].rearrange("p (t e) -> p t e", e=NE),
                                       incl[:].rearrange("p e t -> p t e"), ALU.add))
                for k in range(TOPK):
                    settle(v.tensor_tensor(hot[:, k], hot[:, k], place, ALU.mult))
                settle(v.tensor_reduce(slot[:], hot[:].rearrange("p k t e -> p (k t) e"), mybir.AxisListType.X, ALU.add))
                settle(v.tensor_copy(slot_i[:, 0, :], slot[:]))
                v.tensor_scalar(slot_i[:, 1, :], slot_i[:, 0, :], P - 1, None, ALU.bitwise_and)
                settle(v.tensor_scalar(slot_i[:, 2, :], slot_i[:, 0, :], P.bit_length() - 1, None, ALU.logical_shift_right))
                settle(v.tensor_copy(slot_f[:], slot_i[:, 1:3, :]))
                settle(v.tensor_tensor(high_hot[:, :, 0, :], iota_lane[:, 0:STEPS].unsqueeze(1).to_broadcast([P, NA, STEPS]),
                                       slot_f[:, 1, :].unsqueeze(2).to_broadcast([P, NA, STEPS]), ALU.is_equal))
                v.tensor_scalar(high_hot[:, :, 1, :], high_hot[:, :, 0, :], lane[:, 0:1], None, ALU.mult)
                v.tensor_tensor(high_hot[:, :, 2, :], high_hot[:, :, 0, :],
                                iota_lane[:, 0:NA].unsqueeze(2).to_broadcast([P, NA, STEPS]), ALU.mult)
                for g in range(NG):
                    now = slice(g * NA // NG, (g + 1) * NA // NG)
                    v.tensor_tensor(low_hot[:, now, :], iota_lane[:].unsqueeze(1).to_broadcast([P, NA // NG, P]),
                                    slot_f[:, 0, now].unsqueeze(2).to_broadcast([P, NA // NG, P]), ALU.is_equal)\
                        .then_inc(hot_ready, 1)
                wide = [P, STEPS, NE]
                settle(v.tensor_tensor(past[:], e_end[:].unsqueeze(1).to_broadcast(wide),
                                       iota_lane[:, 0:STEPS].unsqueeze(2).to_broadcast(wide), ALU.is_le))
                settle(v.tensor_reduce(expert_f[:], past[:], mybir.AxisListType.X, ALU.add))
                settle(v.tensor_scalar(expert_f[:], expert_f[:], float(NE - 1), None, ALU.min))
                v.tensor_copy(expert[:], expert_f[:])
                dve.wait_ge(found_ready, r + 1)
                settle(v.tensor_copy(found[:].rearrange("p a n -> p (a n)"), bank[:, 7, 0:3 * STEPS]))
                settle(v.scalar_tensor_tensor(out=dest_f[:], in0=found[:, 2, :], scalar=float(P), in1=found[:, 1, :],
                                              op0=ALU.mult, op1=ALU.add))
                settle(v.tensor_copy(dest[:], dest_f[:]))
                settle(v.tensor_scalar(source[:], dest[:], NT * P - 1, None, ALU.bitwise_and))
                settle(v.tensor_scalar(found[:, 0, :], found[:, 0, :], -float(NOWHERE), float(NOWHERE), ALU.mult, ALU.add))
                settle(v.tensor_tensor(dest_f[:], dest_f[:], found[:, 0, :], ALU.add))
                v.tensor_copy(dest[:], dest_f[:]).then_inc(plan_ready, 1)

                def mul(n, p):
                    dve.wait_ge(silu_done, n + 1 + AHEAD)
                    dve.wait_ge(turn_done, n + 1)
                    v.tensor_tensor(act[:, p, :], bank[:, 2 + p, :], sg[:, p, :], ALU.mult).then_inc(mul_done, 1)

                def take(n, k):
                    dve.wait_ge(row_free, n + 1)
                    dve.wait_ge(down_done, n + 1 + AHEAD)
                    v.tensor_copy(y_row[:, k % RING, :], bank[:, 6, 0:D]).then_inc(y_taken, 1)

                def step(n, k, first=False):
                    mul(n, k % 2)
                    if not first:
                        take(n - 1, k - 1)

                v.scalar_tensor_tensor(out=x[:], in0=hid[:], scalar=0.5, in1=x[:], op0=ALU.mult, op1=ALU.add)\
                    .then_inc(x_halved, 1)
                step(base, 0, first=True)
                with dve.Fori(0, (STEPS - RING) // BODY) as q:
                    for k in range(1, BODY + 1):
                        step(q * BODY + (base + k), k)
                for k in range(STEPS - RING + 1, STEPS):
                    step(base + k, k)
                take(base + STEPS - 1, STEPS - 1)

                dve.wait_ge(x_halved, r + 1)

            def combine(r, g):
                dve.wait_ge(y_back[g], 16 * TOPK * (r + 1))
                for k, src in ((0, normed), (1, x0)):
                    for j in range(GT * g, GT * (g + 1)):
                        ins = v.scalar_tensor_tensor(out=x[:, j, :], in0=src[:, j, :], scalar=w[:, k, j:j + 1],
                                                     in1=x[:, j, :], op0=ALU.mult, op1=ALU.add)
                    settle(ins)
                dve.sem_inc(x_ready, 1)

            dve.sem_inc(mul_done, AHEAD)
            dve.sem_inc(y_taken, 1)
            ffn(0)

            for g in range(NG):
                combine(0, g)
                measure(MAMBA_LN, g, x)
                if g > 0:
                    normalise(MAMBA_LN, g - 1, x, normed)
            normalise(MAMBA_LN, NG - 1, x, normed)
            dve.wait_ge(mamba_in, MAMBA_LOADS)
            def convolve(g):
                dve.wait_ge(u_raw_taken, g + 1)
                for k in range(KC - 1):
                    for h in range(NH):
                        ug = u[:, h, GB * g:GB * (g + 1), :]
                        ins = v.scalar_tensor_tensor(out=ug, in0=u_raw[:, h, GB * g:GB * (g + 1), k:k + L],
                                                     scalar=conv_w[:, h, k:k + 1], in1=ug, op0=ALU.mult, op1=ALU.add)
                    if k < KC - 2:
                        settle(ins)
                ins.then_inc(conv_done, 1)

            def split_bc(g):
                hi = bc_hi[:, bass.ts(g, GW)]
                src = bank[0:96, 1, :]
                dve.wait_ge(bcx_ready, g + 1)
                settle(v.tensor_copy(hi, src))
                settle(v.tensor_tensor(bc_r1, src, hi, ALU.subtract))
                settle(v.tensor_copy(bc_mid[:], bc_r1))
                settle(v.tensor_tensor(bc_r2, bc_r1, bc_mid[:], ALU.subtract))
                v.tensor_copy(hi[32:64, :], bc_mid[32:64, :])
                v.tensor_copy(hi[64:96, :], bc_r2[64:96, :]).then_inc(bc_split, 1)

            convolve(0)
            convolve(1)
            for g in range(NG):
                if g + 2 < NG:
                    convolve(g + 2)
                split_bc(g)
            for g in range(NG):
                dve.wait_ge(exp_ready, g + 1)
                settle(v.tensor_scalar(sp_tmp[g], sp_exp[g], 1.0, 1.0, ALU.add, ALU.subtract))
                settle(v.tensor_tensor(sp_tmp[g], sp_exp[g], sp_tmp[g], ALU.subtract))
            for g in range(NG):
                dve.wait_ge(sp_ready, g + 1)
                settle(v.tensor_tensor(sp_tmp[g], sp_tmp[g], sp_ln[g], ALU.add))
                v.tensor_tensor(sp_relu[g], sp_tmp[g].rearrange("p h (b l) -> p h b l", l=L), sp_relu[g], ALU.add)\
                    .then_inc(dt_ready, 1)
            for i in range(2):
                ins = v.memset(decay[i].rearrange("p h (b l) -> p h b l", l=L)[:, :, :, 0:1], 0.0)
            ins.then_inc(zero_ready, 1)
            dve.sem_inc(scan_done, DRIVES)
            dve.sem_inc(drive_done, B_ROWS)
            dve.sem_inc(read_done, STATES)
            dve.sem_inc(x_added, 1)
            def scan(c, n):
                m = c * NS + n
                dve.wait_ge(read_done, m + 1)
                dve.wait_ge(decay_ready, m + (1 + AHEAD))
                dve.wait_ge(drive_done, m + (1 + B_ROWS))
                v.tensor_tensor_scan(out=state[n % STATES], data0=decay[n % 2].rearrange("p h t -> p (h t)"),
                                     data1=drive[n % DRIVES], initial=0.0, op0=ALU.mult, op1=ALU.add)\
                    .then_inc(scan_done, 1)

            def read_out(c, n):
                m = c * NS + n
                dve.wait_ge(scan_done, m + (1 + DRIVES))
                dve.wait_ge(c_spread, m + 1)
                dve.wait_ge(y_added, m + 1)
                v.tensor_tensor(read[:, n % 2, :].rearrange("p (h t) -> p h t", h=NH),
                                state[n % STATES].rearrange("p (h t) -> p h t", h=NH),
                                bank[:, 7, :].unsqueeze(1).to_broadcast([P, NH, GW]), ALU.mult).then_inc(read_done, 1)

            def chunk(c, last):
                for n in range(1, NS):
                    read_out(c, n)
                    if not (last and n + 2 >= NS):
                        scan(c, n + 2)
                dve.wait_ge(y_added, c * NS + (NS + AHEAD))
                for h in range(NH):
                    uc = u[:, h, bass.ts(c, GB), :].rearrange("p b l -> p (b l)")
                    ins = v.scalar_tensor_tensor(out=yg[:, h, :], in0=uc, scalar=cols[:, 1, h:h + 1],
                                                 in1=bank[:, 4 + h, :], op0=ALU.mult, op1=ALU.add)
                ins.then_inc(y_used, 1)
                dve.wait_ge(y_used, c + 1)
                v.tensor_tensor(yg, yg, zs[:, :, bass.ts(c, GW)], ALU.mult).then_inc(yg_ready, 1)
                if not last:
                    read_out(c, NS)
                    scan(c, NS + 2)
                dve.wait_ge(proj_ready, c + 1)
                xc = x[:, bass.ts(c, GT), :].rearrange("p t d -> p (t d)")
                v.tensor_tensor(xc, bank[:, 4, :], xc, ALU.add).then_inc(x_added, 1)

            scan(0, 0)
            scan(0, 1)
            read_out(0, 0)
            scan(0, 2)
            with dve.Fori(0, NG - 1) as c:
                chunk(c, last=False)
            chunk(NG - 1, last=True)
            dve.wait_ge(x_added, NG + 1)
            ffn(1)
            for g in range(NG):
                combine(1, g)


def kernel(**inputs):
    import numpy as np
    import concourse.bacc as bacc
    from concourse.bass_utils import run_bass_kernel_spmd

    def of(name):
        return np.asarray(inputs["L0_" + name])

    wx = of("attn_W_x").reshape(NH, P, DR + 2 * NS).transpose(1, 0, 2)
    arrays = {
        "x": of("attn_x").reshape(NT * P, D),
        "ln_cols": np.stack([of("ffn_ln1_g"), of("ffn_ln1_b"), of("ffn_ln2_g"), of("ffn_ln2_b")], axis=1),
        "attn_w": of("ffn_attn_w").T,
        "router_w": of("ffn_gate_w").T,
        "gate_w": of("ffn_gate_proj").transpose(2, 0, 1),
        "up_w": of("ffn_up_proj").transpose(2, 0, 1),
        "down_w": of("ffn_down_proj").reshape(NE, D, NI, P).transpose(3, 0, 2, 1),
        "w_in": of("attn_W_in"),
        "conv_w": of("attn_conv_w").reshape(NH, P, KC).transpose(1, 0, 2),
        "cols": np.stack([of("attn_conv_b"), of("attn_D"), of("attn_b_dt")]).reshape(3, NH, P).transpose(2, 0, 1),
        "w_dtlr": wx[:, :, 0:DR],
        "w_bc": np.concatenate([wx[:, :, DR:]] * 3, axis=2),
        "w_dt": of("attn_W_dt"),
        "w_out": of("attn_W_out").reshape(NH, P, D).transpose(1, 0, 2),
        "A_log": of("attn_A_log"),
    }
    arrays = {"in_" + k: np.ascontiguousarray(v) for k, v in arrays.items()}
    nc = bacc.Bacc("TRN2", target_bir_lowering=False, num_devices=1)
    aps = {k[3:]: nc.dram_tensor(k, v.shape, mybir.dt.from_np(v.dtype), kind="ExternalInput").ap()
           for k, v in arrays.items()}
    out = nc.dram_tensor("out", (NT * P, D), F32, kind="ExternalOutput").ap()
    macaron(nc, aps, out)
    r = run_bass_kernel_spmd(nc, [arrays], core_ids=[0])
    return r.results[0]["out"].reshape(NB, L, D)
```
